# Optimizing a Trainium2 kernel written in Bass

```python
import numpy as np
import jax
import jax.numpy as jnp

def _softmax(x, axis=-1):
    return jax.nn.softmax(x, axis=axis)

def _gelu(x):
    return jax.nn.gelu(x, approximate=True)

def _silu(x):
    return jax.nn.silu(x)

def _sigmoid(x):
    return jax.nn.sigmoid(x)

def _layernorm(x, axis=-1, eps=1e-05):
    m = jnp.mean(x, axis=axis, keepdims=True)
    v = jnp.var(x, axis=axis, keepdims=True)
    return (x - m) / jnp.sqrt(v + eps)

def _scatter_add(tgt, idx, src, axis=0):
    return tgt.at[idx].add(src)

def _segment_sum(src, seg, n):
    return jax.ops.segment_sum(src, seg, n)
kernel_name = 'mk_decoder_preln_d1_seqx_r8_86902a'

def setup_inputs(seed: int=0):
    np.random.seed(seed)
    _w = jnp.asarray

    def _rec_inputs():
        import jax
        import jax.numpy as jnp
        _rk = jax.random.key(seed)
        x = -0.000125 + 0.9999 * jax.random.normal(jax.random.fold_in(_rk, 1), (2, 512, 128), jnp.float32)
        _lenS = 512 - jax.random.randint(jax.random.fold_in(_rk, 7), (2,), 0, max(1, 512 // 4) + 1, jnp.int32)
        _lenS2 = 154 - jax.random.randint(jax.random.fold_in(_rk, 8), (2,), 0, max(1, 154 // 4) + 1, jnp.int32)
        _ctx_768P = jax.random.normal(jax.random.fold_in(_rk, 11), (2, 16, 96), jnp.float32)
        _ctx_768c = jax.random.dirichlet(jax.random.fold_in(_rk, 511), 0.3 * jnp.ones((16,), jnp.float32), (2, 154))
        _ctx_768t = jnp.einsum('bsk,bkd->bsd', _ctx_768c, _ctx_768P)
        _ctx_768t = _ctx_768t * jax.lax.rsqrt(jnp.mean(jnp.square(_ctx_768t)) + 1e-12) * 0.953939
        ctx_768 = 0.00272024 + 0.999456 * (_ctx_768t + 0.3 * jax.random.normal(jax.random.fold_in(_rk, 611), (2, 154, 96), jnp.float32))
        return (x, ctx_768)
    x, ctx_768 = _rec_inputs()

    def _L0_attn_setup():
        import jax, jax.numpy as jnp
        import numpy as np
        from jax import lax
        B, S, D_IN = (4, 512, 128)
        D_FAST, D_SLOW = (64, 64)
        Z_BIAS_FAST, Z_BIAS_SLOW = (2.0, -2.0)

        def _binop(q_i, q_j):
            a_i, b_i = q_i
            a_j, b_j = q_j
            return (a_i * a_j, a_j * b_i + b_j)

        def parallel_scan(a, b):
            _, h = lax.associative_scan(_binop, (a, b), axis=1)
            return h
        key = jax.random.key(seed)
        ks = jax.random.split(key, 6)
        scale = 0.02
        x = jax.random.normal(ks[0], (B, S, D_IN), dtype=jnp.float32)
        W_zf = jax.random.normal(ks[1], (D_IN, D_FAST), dtype=jnp.float32) * scale
        b_zf = jnp.full((D_FAST,), Z_BIAS_FAST, dtype=jnp.float32)
        W_hf = jax.random.normal(ks[2], (D_IN, D_FAST), dtype=jnp.float32) * scale
        b_hf = jnp.zeros((D_FAST,), dtype=jnp.float32)
        W_zs = jax.random.normal(ks[3], (D_IN, D_SLOW), dtype=jnp.float32) * scale
        b_zs = jnp.full((D_SLOW,), Z_BIAS_SLOW, dtype=jnp.float32)
        W_hs = jax.random.normal(ks[4], (D_IN, D_SLOW), dtype=jnp.float32) * scale
        b_hs = jnp.zeros((D_SLOW,), dtype=jnp.float32)
        W_g = jax.random.normal(ks[5], (D_FAST + D_SLOW, D_FAST + D_SLOW), dtype=jnp.float32) * scale
        b_g = jnp.zeros((D_FAST + D_SLOW,), dtype=jnp.float32)
        return {'x': x, 'W_zf': W_zf, 'b_zf': b_zf, 'W_hf': W_hf, 'b_hf': b_hf, 'W_zs': W_zs, 'b_zs': b_zs, 'W_hs': W_hs, 'b_hs': b_hs, 'W_g': W_g, 'b_g': b_g}
    _L0_attn_all = _L0_attn_setup()
    _L0_attn_in = {k: v for k, v in _L0_attn_all.items() if k in ('W_zf', 'b_zf', 'W_hf', 'b_hf', 'W_zs', 'b_zs', 'W_hs', 'b_hs', 'W_g', 'b_g')}
    del _L0_attn_all

    def _L0_xattn_setup():
        import jax, jax.numpy as jnp
        import numpy as np
        QUERY_DIM = 128
        CONTEXT_DIM = 96
        HEADS = 8
        DIM_HEAD = 64
        INNER = HEADS * DIM_HEAD
        key = jax.random.key(seed)
        ks = jax.random.split(key, 7)
        B, S, L = (8, 512, 77)
        x = jax.random.normal(ks[0], (B, S, QUERY_DIM), dtype=jnp.float32)
        context = jax.random.normal(ks[1], (B, L, CONTEXT_DIM), dtype=jnp.float32)
        Wq = jax.random.normal(ks[2], (QUERY_DIM, INNER), dtype=jnp.float32) * QUERY_DIM ** (-0.5)
        Wk = jax.random.normal(ks[3], (CONTEXT_DIM, INNER), dtype=jnp.float32) * CONTEXT_DIM ** (-0.5)
        Wv = jax.random.normal(ks[4], (CONTEXT_DIM, INNER), dtype=jnp.float32) * CONTEXT_DIM ** (-0.5)
        Wo = jax.random.normal(ks[5], (INNER, QUERY_DIM), dtype=jnp.float32) * INNER ** (-0.5)
        bo = jax.random.normal(ks[6], (QUERY_DIM,), dtype=jnp.float32) * 0.01
        return {'x': x, 'context': context, 'Wq': Wq, 'Wk': Wk, 'Wv': Wv, 'Wo': Wo, 'bo': bo}
    _L0_xattn_all = _L0_xattn_setup()
    _L0_xattn_in = {k: v for k, v in _L0_xattn_all.items() if k in ('Wq', 'Wk', 'Wv', 'Wo', 'bo')}
    del _L0_xattn_all

    def _L0_ffn_setup():
        import jax, jax.numpy as jnp
        import numpy as np
        EXPERTS = 8
        TOP_K = 2

        def swiglu(x, w1, w2, w3):
            h = x @ w1
            return h * jax.nn.sigmoid(h) * (x @ w2) @ w3
        key = jax.random.key(seed)
        ks = jax.random.split(key, 9)
        B, S, D = (4, 256, 128)
        H = 2 * D
        s = 0.02
        x = jax.random.normal(ks[0], (B, S, D), dtype=jnp.float32)
        gate_w = jax.random.normal(ks[1], (D, EXPERTS), dtype=jnp.float32) * s
        ew1 = jax.random.normal(ks[2], (EXPERTS, D, H), dtype=jnp.float32) * s
        ew2 = jax.random.normal(ks[3], (EXPERTS, D, H), dtype=jnp.float32) * s
        ew3 = jax.random.normal(ks[4], (EXPERTS, H, D), dtype=jnp.float32) * s
        sw1 = jax.random.normal(ks[5], (D, H), dtype=jnp.float32) * s
        sw2 = jax.random.normal(ks[6], (D, H), dtype=jnp.float32) * s
        sw3 = jax.random.normal(ks[7], (H, D), dtype=jnp.float32) * s
        return {'x': x, 'gate_w': gate_w, 'ew1': ew1, 'ew2': ew2, 'ew3': ew3, 'sw1': sw1, 'sw2': sw2, 'sw3': sw3}
    _L0_ffn_all = _L0_ffn_setup()
    _L0_ffn_in = {k: v for k, v in _L0_ffn_all.items() if k in ('gate_w', 'ew1', 'ew2', 'ew3', 'sw1', 'sw2', 'sw3')}
    del _L0_ffn_all
    return {'x': x, 'ctx_768': ctx_768, 'L0_attn_W_zf': _L0_attn_in['W_zf'], 'L0_attn_b_zf': _L0_attn_in['b_zf'], 'L0_attn_W_hf': _L0_attn_in['W_hf'], 'L0_attn_b_hf': _L0_attn_in['b_hf'], 'L0_attn_W_zs': _L0_attn_in['W_zs'], 'L0_attn_b_zs': _L0_attn_in['b_zs'], 'L0_attn_W_hs': _L0_attn_in['W_hs'], 'L0_attn_b_hs': _L0_attn_in['b_hs'], 'L0_attn_W_g': _L0_attn_in['W_g'], 'L0_attn_b_g': _L0_attn_in['b_g'], 'L0_xattn_Wq': _L0_xattn_in['Wq'], 'L0_xattn_Wk': _L0_xattn_in['Wk'], 'L0_xattn_Wv': _L0_xattn_in['Wv'], 'L0_xattn_Wo': _L0_xattn_in['Wo'], 'L0_xattn_bo': _L0_xattn_in['bo'], 'L0_ffn_gate_w': _L0_ffn_in['gate_w'], 'L0_ffn_ew1': _L0_ffn_in['ew1'], 'L0_ffn_ew2': _L0_ffn_in['ew2'], 'L0_ffn_ew3': _L0_ffn_in['ew3'], 'L0_ffn_sw1': _L0_ffn_in['sw1'], 'L0_ffn_sw2': _L0_ffn_in['sw2'], 'L0_ffn_sw3': _L0_ffn_in['sw3']}

def reference(x, ctx_768, L0_attn_W_zf, L0_attn_b_zf, L0_attn_W_hf, L0_attn_b_hf, L0_attn_W_zs, L0_attn_b_zs, L0_attn_W_hs, L0_attn_b_hs, L0_attn_W_g, L0_attn_b_g, L0_xattn_Wq, L0_xattn_Wk, L0_xattn_Wv, L0_xattn_Wo, L0_xattn_bo, L0_ffn_gate_w, L0_ffn_ew1, L0_ffn_ew2, L0_ffn_ew3, L0_ffn_sw1, L0_ffn_sw2, L0_ffn_sw3):
    import jax
    import jax.numpy as jnp

    def _L0_attn_ref(x, W_zf, b_zf, W_hf, b_hf, W_zs, b_zs, W_hs, b_hs, W_g, b_g):
        import jax, jax.numpy as jnp
        import numpy as np
        from jax import lax
        B, S, D_IN = (4, 512, 128)
        D_FAST, D_SLOW = (64, 64)
        Z_BIAS_FAST, Z_BIAS_SLOW = (2.0, -2.0)

        def _binop(q_i, q_j):
            a_i, b_i = q_i
            a_j, b_j = q_j
            return (a_i * a_j, a_j * b_i + b_j)

        def parallel_scan(a, b):
            _, h = lax.associative_scan(_binop, (a, b), axis=1)
            return h
        z_fast = jax.nn.sigmoid(jnp.einsum('bsd,df->bsf', x, W_zf) + b_zf)
        h_tilde_fast = jnp.einsum('bsd,df->bsf', x, W_hf) + b_hf
        h_fast = parallel_scan(1.0 - z_fast, z_fast * h_tilde_fast)
        z_slow = jax.nn.sigmoid(jnp.einsum('bsd,df->bsf', x, W_zs) + b_zs)
        h_tilde_slow = jnp.einsum('bsd,df->bsf', x, W_hs) + b_hs
        h_slow = parallel_scan(1.0 - z_slow, z_slow * h_tilde_slow)
        h_combined = jnp.concatenate([h_fast, h_slow], axis=-1)
        gate = jax.nn.sigmoid(jnp.einsum('bsc,cd->bsd', h_combined, W_g) + b_g)
        return gate * h_combined

    def _L0_xattn_ref(x, context, Wq, Wk, Wv, Wo, bo):
        import jax, jax.numpy as jnp
        import numpy as np
        QUERY_DIM = 128
        CONTEXT_DIM = 96
        HEADS = 8
        DIM_HEAD = 64
        INNER = HEADS * DIM_HEAD
        B, S, _ = x.shape
        L = context.shape[1]
        scale = DIM_HEAD ** (-0.5)
        q = (x @ Wq).reshape(B, S, HEADS, DIM_HEAD).transpose(0, 2, 1, 3)
        k = (context @ Wk).reshape(B, L, HEADS, DIM_HEAD).transpose(0, 2, 1, 3)
        v = (context @ Wv).reshape(B, L, HEADS, DIM_HEAD).transpose(0, 2, 1, 3)
        attn = jnp.einsum('bhsd,bhld->bhsl', q, k) * scale
        attn = jax.nn.softmax(attn, axis=-1)
        out = jnp.einsum('bhsl,bhld->bhsd', attn, v)
        out = out.transpose(0, 2, 1, 3).reshape(B, S, INNER)
        return out @ Wo + bo

    def _L0_ffn_ref(x, gate_w, ew1, ew2, ew3, sw1, sw2, sw3):
        import jax, jax.numpy as jnp
        import numpy as np
        EXPERTS = 8
        TOP_K = 2

        def swiglu(x, w1, w2, w3):
            h = x @ w1
            return h * jax.nn.sigmoid(h) * (x @ w2) @ w3
        B, S, D = x.shape
        gate_out = x @ gate_w
        top_v, top_i = jax.lax.top_k(gate_out, TOP_K)
        masked = jnp.full_like(gate_out, -1e+20)
        bi = jnp.arange(B)[:, None, None]
        si = jnp.arange(S)[None, :, None]
        masked = masked.at[bi, si, top_i].set(top_v)
        probs = jax.nn.softmax(masked, axis=-1)
        chosen = jnp.zeros_like(gate_out, dtype=bool).at[bi, si, top_i].set(True)
        w = jnp.where(chosen, probs, 0.0)

        def one_expert(w1, w2, w3, we):
            return swiglu(x, w1, w2, w3) * we[..., None]
        out = jax.vmap(one_expert, in_axes=(0, 0, 0, 2))(ew1, ew2, ew3, w).sum(0)
        out = out + swiglu(x, sw1, sw2, sw3)
        return out
    x = x + _L0_attn_ref(_layernorm(x, axis=-1), L0_attn_W_zf, L0_attn_b_zf, L0_attn_W_hf, L0_attn_b_hf, L0_attn_W_zs, L0_attn_b_zs, L0_attn_W_hs, L0_attn_b_hs, L0_attn_W_g, L0_attn_b_g)
    x = x + _L0_xattn_ref(_layernorm(x, axis=-1), ctx_768, L0_xattn_Wq, L0_xattn_Wk, L0_xattn_Wv, L0_xattn_Wo, L0_xattn_bo)
    x = x + _L0_ffn_ref(_layernorm(x, axis=-1), L0_ffn_gate_w, L0_ffn_ew1, L0_ffn_ew2, L0_ffn_ew3, L0_ffn_sw1, L0_ffn_sw2, L0_ffn_sw3)
    return x

_drawn_inputs = setup_inputs


def setup_inputs(seed=0):
    import zlib

    import numpy as np

    out = dict(_drawn_inputs(seed))
    spreads = {'L0_attn_b_zf': (2.0, 0.6),
     'L0_attn_b_hf': (0.0, 0.1),
     'L0_attn_b_zs': (-2.0, 0.6),
     'L0_attn_b_hs': (0.0, 0.1),
     'L0_attn_b_g': (0.0, 0.8)}
    factors = {'L0_attn_W_zf': 8.0,
     'L0_attn_W_zs': 8.0,
     'L0_attn_W_hs': 2.998,
     'L0_attn_W_g': 8.0,
     'L0_xattn_bo': 6.136,
     'L0_ffn_gate_w': 8.0,
     'L0_ffn_ew1': 8.0,
     'L0_ffn_ew2': 8.0,
     'L0_ffn_ew3': 8.0,
     'L0_ffn_sw1': 8.0,
     'L0_ffn_sw2': 7.837,
     'L0_ffn_sw3': 7.915}
    for name, (base, spread) in spreads.items():
        noise = np.random.default_rng([zlib.crc32(name.encode()), seed]).standard_normal(out[name].shape)
        drawn = base * np.exp(spread * noise) if base else spread * noise
        out[name] = jnp.asarray(drawn.astype(out[name].dtype))
    for name, factor in factors.items():
        out[name] = (out[name] * factor).astype(out[name].dtype)
    return out
```

```python
from contextlib import ExitStack

import concourse.bass as bass
from concourse import mybir

F32 = mybir.dt.float32
BF16 = mybir.dt.bfloat16
U32 = mybir.dt.uint32
ALU = mybir.AluOpType
ACT = mybir.ActivationFunctionType
AX_X = mybir.AxisListType.X

P = 128
D = 128
BATCH, SEQ = 2, 512
TOK = BATCH * SEQ
TILES = TOK // P
TPB = SEQ // P
CH = 64
CTX, CL = 96, 154
CTX_ROWS = BATCH * CL
HEADS, DH = 8, 64
INNER = HEADS * DH
HL = HEADS * CL
NCH = (HL + P - 1) // P
HPU = 4
E, H = 8, 256
HC = H // P
UPE = BATCH * HC
EPS = 1e-5
CTX_CUTS = [(0, P), (P, P), (2 * P, CTX_ROWS - 2 * P)]
GROUPS = [(0, 4), (4, 4), (8, NCH - 8)]


def rows_of(c):
    return min(P, HL - c * P)


def decoder_block(nc, x, ctx_in, w_zf, b_zf, w_hf, b_hf, w_zs, b_zs, w_hs, b_hs, w_g, b_g,
                  w_q, w_k, w_v, w_o, b_o, w_gate, ew1, ew2, ew3, sw1, sw2, sw3, scratch, out):
    with ExitStack() as ctx:
        def sb(name, shape, dt=F32):
            return ctx.enter_context(nc.sbuf_tensor(name, shape, dt))

        def sem(name):
            return ctx.enter_context(nc.semaphore(name))

        bank = [ctx.enter_context(nc.psum_tensor(f"bank{i}", [P, 512], F32)) for i in range(8)]

        ident = sb("ident", [P, P])
        minus_half = sb("minus_half", [P, TILES])
        zeros = sb("zeros", [1, 512], BF16)
        expert_ids = sb("expert_ids", [P, E])
        x_tok = sb("x_tok", [P, TILES, D])
        xn = sb("xn", [P, TILES, D])
        stats = sb("stats", [P, TILES, 6])
        moments = sb("moments", [P, TILES, 2])
        var_eps = sb("var_eps", [P, TILES])
        rstd = sb("rstd", [P, TILES])
        xnT = sb("xnT", [P, TOK])
        wz, wh, wg = sb("wz", [P, P]), sb("wh", [P, P]), sb("wg", [P, P])
        bz, bh, bg = sb("bz", [P, 1]), sb("bh", [P, 1]), sb("bg", [P, 1])
        zT, decayT, driveT = sb("zT", [P, TOK]), sb("decayT", [P, TOK]), sb("driveT", [P, TOK])
        hT, gateT, yT = sb("hT", [P, TOK]), sb("gateT", [P, TOK]), sb("yT", [P, TOK])
        ctx_rows = sb("ctx_rows", [P, 3, CTX])
        ctxT = sb("ctxT", [CTX, CTX_ROWS])
        wq, wk, wv = sb("wq", [P, INNER]), sb("wk", [CTX, INNER]), sb("wv", [CTX, INNER])
        wo = sb("wo", [P, 4, D])
        wqT = sb("wqT", [P, 4, D])
        kT, vT = sb("kT", [P, 4, CTX_ROWS]), sb("vT", [P, 4, CTX_ROWS])
        A = sb("A", [P, BATCH, HEADS, CL])
        UT = sb("UT", [P, BATCH, HEADS, CL])
        U = sb("U", [P, BATCH, NCH, D])
        bo_rows = sb("bo_rows", [P, D])
        probs = sb("probs", [P, 3, HEADS, CL])
        neg_max = sb("neg_max", [P, 2 * TILES, HPU])
        row_sum = sb("row_sum", [P, 2 * TILES, HPU])
        inv_sum = sb("inv_sum", [P, 2 * TILES, HPU])
        probsT = sb("probsT", [P, 2, NCH, P])
        gate_w = sb("gate_w", [P, E])
        logits = sb("logits", [P, TILES, E])
        top_v = sb("top_v", [P, TILES, 8])
        top_i = sb("top_i", [P, TILES, 8], U32)
        gap = sb("gap", [P, TILES])
        second = sb("second", [P, TILES])
        norm1, p1, p2 = sb("norm1", [P, TILES]), sb("p1", [P, TILES]), sb("p2", [P, TILES])
        mask1, mask2 = sb("mask1", [P, E, TILES]), sb("mask2", [P, E, TILES])
        w_tok = sb("w_tok", [P, E, TILES])
        w_rows = sb("w_rows", [E * TILES, P])
        share = [sb(f"share{p}", [P, TOK]) for p in range(2)]
        w1s = [sb(f"w1s{p}", [P, H]) for p in range(2)]
        w2s = [sb(f"w2s{p}", [P, H]) for p in range(2)]
        w3s = [sb(f"w3s{p}", [P, HC, D]) for p in range(2)]
        sil, prod = sb("sil", [P, 2, 512]), sb("prod", [P, 2, 512])
        hidden = sb("hidden", [P, UPE, 512])
        moeT = sb("moeT", [P, TOK])
        out_tok = sb("out_tok", [P, TILES, D])

        x_in = [sem(f"x_in{b}") for b in range(BATCH)]
        wzh_in, wg_in, ctx_in_s, wqk_in, wvo_in, bo_in, gw_in = (
            sem(n) for n in ("wzh_in", "wg_in", "ctx_in", "wqk_in", "wvo_in", "bo_in", "gw_in"))
        consts = sem("consts")
        dve_step = sem("dve_step")
        var_ready, rstd_ready, xn_ready = sem("var_ready"), sem("rstd_ready"), sem("xn_ready")
        xt_mm, xt_evac = sem("xt_mm"), sem("xt_evac")
        z_mm, hh_mm, z_ready, scan_ready, drive_ready = (
            sem(n) for n in ("z_mm", "hh_mm", "z_ready", "scan_ready", "drive_ready"))
        gate_mm, gate_ready, y_ready, ytok_mm, x1_ready = (
            sem(n) for n in ("gate_mm", "gate_ready", "y_ready", "ytok_mm", "x1_ready"))
        prep_mm, prep_evac = sem("prep_mm"), sem("prep_evac")
        s_mm, max_ready, exp_done, inv_ready, pn_ready = (
            sem(n) for n in ("s_mm", "max_ready", "exp_done", "inv_ready", "pn_ready"))
        pt_mm, pt_evac, pv_mm, x2_ready, xt3_mm, xt3_evac = (
            sem(n) for n in ("pt_mm", "pt_evac", "pv_mm", "x2_ready", "xt3_mm", "xt3_evac"))
        logit_mm, logit_read, gap_ready, second_ready = (
            sem(n) for n in ("logit_mm", "logit_read", "gap_ready", "second_ready"))
        w_tok_ready, w_mm, w_rows_ready, w_stored = (
            sem(n) for n in ("w_tok_ready", "w_mm", "w_rows_ready", "w_stored"))
        share_in = [sem(f"share_in{p}") for p in range(2)]
        ew_in = [sem(f"ew_in{p}") for p in range(2)]
        h1_mm, h2_mm, o_mm, sil_ready, prod_ready, hid_ready = (
            sem(n) for n in ("h1_mm", "h2_mm", "o_mm", "sil_ready", "prod_ready", "hid_ready"))
        moe_evac, fin_mm, out_ready, stored = (
            sem(n) for n in ("moe_evac", "fin_mm", "out_ready", "stored"))

        x_view = x.rearrange("b (t p) d -> b p t d", p=P)
        out_view = out.rearrange("b (t p) d -> b p t d", p=P)
        ctx_view = ctx_in.rearrange("b l c -> (b l) c")
        col = lambda v: v.rearrange("(n a) -> n a", a=1)
        row = lambda v: v.rearrange("(a n) -> a n", a=1)

        block = ctx.enter_context(nc.Block())

        @block.sync
        def _(sp):
            def load_expert(p, a1, a2, a3):
                sp.dma_start(w1s[p][:], a1).then_inc(ew_in[p], 16)
                sp.dma_start(w2s[p][:], a2).then_inc(ew_in[p], 16)
                sp.dma_start(w3s[p][:], a3.rearrange("(c p) n -> p c n", p=P)).then_inc(ew_in[p], 16)

            def load_share(p, e):
                sp.dma_start(share[p][:], scratch[bass.ds(e, 1), :].broadcast_to([P, TOK])).then_inc(share_in[p], 16)

            for b in range(BATCH):
                sp.dma_start(x_tok[:, b * TPB:(b + 1) * TPB, :], x_view[b]).then_inc(x_in[b], 16)
            sp.dma_start(wz[:, 0:CH], w_zf).then_inc(wzh_in, 16)
            sp.dma_start(wz[:, CH:P], w_zs).then_inc(wzh_in, 16)
            sp.dma_start(wh[:, 0:CH], w_hf).then_inc(wzh_in, 16)
            sp.dma_start(wh[:, CH:P], w_hs).then_inc(wzh_in, 16)
            sp.dma_start(bz[0:CH, :], col(b_zf)).then_inc(wzh_in, 16)
            sp.dma_start(bz[CH:P, :], col(b_zs)).then_inc(wzh_in, 16)
            sp.dma_start(bh[0:CH, :], col(b_hf)).then_inc(wzh_in, 16)
            sp.dma_start(bh[CH:P, :], col(b_hs)).then_inc(wzh_in, 16)
            sp.dma_start(wg[:], w_g).then_inc(wg_in, 16)
            sp.dma_start(bg[:], col(b_g)).then_inc(wg_in, 16)
            sp.dma_start(bo_rows[:], row(b_o).broadcast_to([P, D])).then_inc(bo_in, 16)
            sp.dma_start(gate_w[:], w_gate).then_inc(gw_in, 16)
            load_expert(1, sw1, sw2, sw3)
            load_expert(0, ew1[0], ew2[0], ew3[0])
            sp.wait_ge(w_rows_ready, 1)
            sp.dma_start(scratch.rearrange("e (t p) -> (e t) p", p=P), w_rows[:]).then_inc(w_stored, 16)
            sp.wait_ge(w_stored, 16)
            load_share(0, 0)
            with sp.Fori(0, E // 2 - 1) as i:
                sp.wait_ge(h2_mm, 8 * i + 4)
                sp.wait_ge(o_mm, 8 * i + 4)
                e = 2 * i + 1
                load_expert(1, ew1[e], ew2[e], ew3[e])
                load_share(1, e)
                sp.wait_ge(h2_mm, 8 * i + 8)
                sp.wait_ge(o_mm, 8 * i + 8)
                load_expert(0, ew1[e + 1], ew2[e + 1], ew3[e + 1])
                load_share(0, e + 1)
            sp.wait_ge(h2_mm, 8 * (E // 2 - 1) + 4)
            sp.wait_ge(o_mm, 8 * (E // 2 - 1) + 4)
            load_expert(1, ew1[E - 1], ew2[E - 1], ew3[E - 1])
            load_share(1, E - 1)
            for b in range(BATCH):
                sp.wait_ge(out_ready, b + 1)
                sp.dma_start(out_view[b], out_tok[:, b * TPB:(b + 1) * TPB, :]).then_inc(stored, 16)
            sp.wait_ge(stored, 16 * BATCH)

        @block.gpsimd
        def _(pool):
            nc.gpsimd.memset(ident[:], 0.0).then_inc(consts, 1)
            nc.gpsimd.memset(minus_half[:], -0.5).then_inc(consts, 1)
            nc.gpsimd.iota(expert_ids[:], pattern=[[1, E]], base=0, channel_multiplier=0,
                           allow_small_or_imprecise_dtypes=True).then_inc(consts, 1)
            nc.gpsimd.memset(zeros[:], 0.0).then_inc(consts, 1)
            pool.wait_ge(consts, 4)
            nc.gpsimd.affine_select(out=ident[:], in_=ident[:], compare_op=ALU.not_equal, fill=1.0,
                                    base=0, pattern=[[-1, P]], channel_multiplier=1).then_inc(consts, 1)
            pool.wait_ge(consts, 5)

            def rsqrt(n, t0, t1):
                pool.wait_ge(var_ready, n + 1)
                nc.gpsimd.tensor_tensor(rstd[:, t0:t1], var_eps[:, t0:t1], minus_half[:, t0:t1],
                                        ALU.pow).then_inc(rstd_ready, 1)

            for n in range(2 * BATCH):
                b = n % BATCH
                rsqrt(n, b * TPB, (b + 1) * TPB)

            def normalise(t, hh):
                s = 2 * t + hh
                pool.wait_ge(inv_ready, s + 1)
                view = probs[:, t % 3, hh * HPU:(hh + 1) * HPU, :]
                nc.gpsimd.tensor_tensor(view, view, inv_sum[:, s, :].unsqueeze(2).broadcast_to([P, HPU, CL]),
                                        ALU.mult).then_inc(pn_ready, 1)

            normalise(0, 0)
            normalise(0, 1)
            normalise(1, 0)
            for t in range(TILES):
                if t >= 1:
                    rsqrt(2 * BATCH + t - 1, t - 1, t)
                if t + 1 < TILES:
                    normalise(t + 1, 1)
                if t + 2 < TILES:
                    normalise(t + 2, 0)
            rsqrt(2 * BATCH + TILES - 1, TILES - 1, TILES)

            for u in range(UPE):
                pool.wait_ge(prod_ready, u + 1)
                nc.gpsimd.tensor_copy(hidden[:, u, :], prod[:, u % 2, :]).then_inc(hid_ready, 1)
            with pool.Fori(0, E // 2) as i:
                for k in range(2 * UPE):
                    u = 8 * i + (UPE + k)
                    if k % UPE == 0:
                        pool.wait_ge(share_in[k // UPE], 16 * i + 16)
                    pool.wait_ge(prod_ready, u + 1)
                    pool.wait_ge(o_mm, u - 3)
                    n = k % UPE // HC
                    nc.gpsimd.tensor_tensor(
                        hidden[:, k % UPE, :], prod[:, k % 2, :],
                        share[k // UPE][:, n * SEQ:(n + 1) * SEQ], ALU.mult).then_inc(hid_ready, 1)

        @block.scalar
        def _(act):
            act.dma_start(wk[:], w_k).then_inc(wqk_in, 16)
            for c, (r0, n) in enumerate(CTX_CUTS):
                act.dma_start(ctx_rows[0:n, c, :], ctx_view[r0:r0 + n, :]).then_inc(ctx_in_s, 16)
            act.dma_start(wq[:], w_q).then_inc(wqk_in, 16)
            act.dma_start(wv[:], w_v).then_inc(wvo_in, 16)
            act.dma_start(wo[:], w_o.rearrange("(c p) n -> p c n", p=P)).then_inc(wvo_in, 16)

            def prep(r, dst, src, scale=1.0):
                act.wait_ge(prep_mm, r + 1)
                nc.scalar.activation(dst, src, ACT.Copy, scale=scale).then_inc(prep_evac, 1)

            def by_batch(ap):
                return ap.rearrange("p (b l) -> p b l", b=BATCH)

            def evac_xt(n, b):
                act.wait_ge(xt_mm, n + 1)
                nc.scalar.activation(xnT[:, b * SEQ:(b + 1) * SEQ], bank[4 + b][:], ACT.Copy).then_inc(xt_evac, 1)

            def forget_gate(b):
                act.wait_ge(z_mm, b + 1)
                nc.scalar.activation(zT[:, b * SEQ:(b + 1) * SEQ], bank[6][:], ACT.Sigmoid,
                                     bias=bz[:, 0:1]).then_inc(z_ready, 1)

            def out_gate(b):
                act.wait_ge(gate_mm, b + 1)
                nc.scalar.activation(gateT[:, b * SEQ:(b + 1) * SEQ], bank[2][:], ACT.Sigmoid,
                                     bias=bg[:, 0:1]).then_inc(gate_ready, 1)

            prep(0, ctxT[:], bank[0][0:CTX, 0:CTX_ROWS])
            prep(1, wqT[:].rearrange("p c d -> p (c d)"), bank[1][:])
            for c in range(4):
                prep(2 + c, kT[:, c, :], bank[c % 2][:, 0:CTX_ROWS])
            act.wait_ge(wzh_in, 16 * 8)
            evac_xt(0, 0)
            forget_gate(0)
            for c in range(4):
                prep(6 + c, vT[:, c, :], bank[c % 2][:, 0:CTX_ROWS])
            evac_xt(1, 1)
            forget_gate(1)
            for h in range(4):
                prep(10 + h, A[:, :, h, :], by_batch(bank[h % 2][:, 0:CTX_ROWS]), scale=DH ** -0.5)
            act.wait_ge(wg_in, 32)
            out_gate(0)
            for h in range(4, 8):
                prep(10 + h, A[:, :, h, :], by_batch(bank[h % 2][:, 0:CTX_ROWS]), scale=DH ** -0.5)
            out_gate(1)
            for h in range(8):
                prep(18 + h, UT[:, :, h, :], by_batch(bank[h % 2][:, 0:CTX_ROWS]))
            for b in range(BATCH):
                evac_xt(2 + b, b)
                for g, (c0, n) in enumerate(GROUPS):
                    r = 26 + 3 * b + g
                    src = bank[r % 2]
                    if g < 2:
                        prep(r, U[:, b, c0:c0 + n, :], src[:].rearrange("p (c d) -> p c d", d=D))
                    else:
                        act.wait_ge(prep_mm, r + 1)
                        nc.scalar.activation(U[:, b, 8, :], src[:, 0:D], ACT.Copy)
                        nc.scalar.activation(U[0:rows_of(9), b, 9, :], src[0:rows_of(9), D:2 * D],
                                             ACT.Copy).then_inc(prep_evac, 1)

            def exps(t, hh):
                s = 2 * t + hh
                act.wait_ge(max_ready, s + 1)
                if t >= 3:
                    act.wait_ge(pt_mm, 3 * (t - 2))
                for q in range(HPU):
                    ins = nc.scalar.activation(probs[:, t % 3, hh * HPU + q, :],
                                               bank[2 * hh + q // 2][:, (q % 2) * CL:(q % 2 + 1) * CL], ACT.Exp,
                                               bias=neg_max[:, s, q:q + 1], accum_out=row_sum[:, s, q:q + 1])
                ins.then_inc(exp_done, 1)

            def evac_xt3(t):
                act.wait_ge(xt3_mm, t + 1)
                nc.scalar.activation(xnT[:, t * P:(t + 1) * P], bank[4][:, 0:P], ACT.Copy).then_inc(xt3_evac, 1)

            for s in range(4):
                exps(s // 2, s % 2)
            for t in range(TILES):
                if t + 2 < TILES:
                    exps(t + 2, 0)
                if t >= 1:
                    evac_xt3(t - 1)
                if t + 2 < TILES:
                    exps(t + 2, 1)
            evac_xt3(TILES - 1)
            act.wait_ge(gap_ready, 1)
            nc.scalar.activation(second[:], gap[:], ACT.Exp).then_inc(second_ready, 1)

            def silu(u, k):
                act.wait_ge(h1_mm, u + 1)
                nc.scalar.activation(sil[:, k % 2, :], bank[k % 2][:], ACT.Silu).then_inc(sil_ready, 1)

            for u in range(UPE):
                if u >= 2:
                    act.wait_ge(prod_ready, u - 1)
                silu(u, u)
            with act.Fori(0, E // 2) as i:
                for k in range(2 * UPE):
                    u = 8 * i + (UPE + k)
                    act.wait_ge(prod_ready, u - 1)
                    silu(u, k)
            for b in range(BATCH):
                act.wait_ge(o_mm, (E + 1) * UPE - 2 + 2 * b if b else (E + 1) * UPE - 2)
                nc.scalar.activation(moeT[:, b * SEQ:(b + 1) * SEQ], bank[6 + b][:], ACT.Copy).then_inc(moe_evac, 1)

        @block.vector
        def _(dve):
            steps = [0]

            def step(ins):
                steps[0] += 1
                ins.then_inc(dve_step, 1)

            def settle():
                dve.wait_ge(dve_step, steps[0])

            def moments_of(t0, t1):
                for t in range(t0, t1):
                    step(nc.vector.bn_stats(stats[:, t, :], x_tok[:, t, :]))
                settle()
                for t in range(t0, t1):
                    step(nc.vector.bn_aggr(moments[:, t, :], stats[:, t, :]))
                settle()
                nc.vector.tensor_scalar(var_eps[:, t0:t1], moments[:, t0:t1, 1], EPS, None,
                                        ALU.add).then_inc(var_ready, 1)

            def normalise(n, t0, t1):
                dve.wait_ge(rstd_ready, n + 1)
                for t in range(t0, t1):
                    ins = nc.vector.tensor_scalar(xn[:, t, :], x_tok[:, t, :], moments[:, t, 0:1],
                                                  rstd[:, t:t + 1], ALU.subtract, ALU.mult)
                ins.then_inc(xn_ready, 1)

            def half(b):
                return slice(b * SEQ, (b + 1) * SEQ)

            for b in range(BATCH):
                dve.wait_ge(x_in[b], 16)
                moments_of(b * TPB, (b + 1) * TPB)
            for b in range(BATCH):
                normalise(b, b * TPB, (b + 1) * TPB)
            dve.wait_ge(wzh_in, 16 * 8)
            for b in range(BATCH):
                dve.wait_ge(z_ready, b + 1)
                step(nc.vector.tensor_scalar(decayT[:, half(b)], zT[:, half(b)], -1.0, 1.0, ALU.mult, ALU.add))
                dve.wait_ge(hh_mm, b + 1)
                step(nc.vector.scalar_tensor_tensor(driveT[:, half(b)], bank[7][:], bh[:, 0:1], zT[:, half(b)],
                                                    ALU.add, ALU.mult))
                settle()
                nc.vector.tensor_tensor_scan(hT[:, half(b)], decayT[:, half(b)], driveT[:, half(b)], 0.0,
                                             ALU.mult, ALU.add).then_inc(scan_ready, 1)

            def gated(b):
                dve.wait_ge(gate_ready, b + 1)
                dve.wait_ge(scan_ready, b + 1)
                nc.vector.tensor_tensor(yT[:, half(b)], gateT[:, half(b)], hT[:, half(b)],
                                        ALU.mult).then_inc(y_ready, 1)

            def residual1(b):
                tiles = slice(b * TPB, (b + 1) * TPB)
                dve.wait_ge(ytok_mm, b + 1)
                nc.vector.tensor_tensor(x_tok[:, tiles, :], x_tok[:, tiles, :],
                                        bank[3][:].rearrange("p (t d) -> p t d", d=D), ALU.add).then_inc(x1_ready, 1)
                dve.wait_ge(x1_ready, b + 1)
                moments_of(b * TPB, (b + 1) * TPB)

            gated(0)
            residual1(0)
            gated(1)
            normalise(2, 0, TPB)
            residual1(1)
            normalise(3, TPB, TILES)
            dve.wait_ge(bo_in, 16)
            dve.wait_ge(xn_ready, 4)
            step(nc.vector.tensor_tensor(x_tok[:], x_tok[:], bo_rows[:].unsqueeze(1).broadcast_to([P, TILES, D]), ALU.add))
            settle()

            def row_max(t, hh):
                s = 2 * t + hh
                dve.wait_ge(s_mm, s + 1)
                for j in range(2):
                    ins = nc.vector.tensor_reduce(neg_max[:, s, 2 * j:2 * j + 2],
                                                  bank[2 * hh + j][:, 0:2 * CL].rearrange("p (h l) -> p h l", l=CL),
                                                  AX_X, ALU.max, negate=True)
                ins.then_inc(max_ready, 1)

            def inverse(t, hh):
                s = 2 * t + hh
                dve.wait_ge(exp_done, s + 1)
                nc.vector.reciprocal(inv_sum[:, s, :], row_sum[:, s, :]).then_inc(inv_ready, 1)

            def evac_pt(t, g):
                c0, n = GROUPS[g]
                dve.wait_ge(pt_mm, 3 * t + g + 1)
                if g == 0 and t >= 2:
                    dve.wait_ge(pv_mm, t - 1)
                src = bank[4 if g == 0 else 5]
                if g < 2:
                    nc.vector.tensor_copy(probsT[:, t % 2, c0:c0 + n, :],
                                          src[:].rearrange("p (c d) -> p c d", d=P)).then_inc(pt_evac, 1)
                else:
                    step(nc.vector.tensor_copy(probsT[:, t % 2, 8, :], src[:, 0:P]))
                    nc.vector.tensor_copy(probsT[0:rows_of(9), t % 2, 9, :],
                                          src[0:rows_of(9), P:2 * P]).then_inc(pt_evac, 1)

            def residual2(t):
                dve.wait_ge(pv_mm, t + 1)
                nc.vector.tensor_tensor(x_tok[:, t, :], x_tok[:, t, :], bank[6 + t % 2][:, 0:D],
                                        ALU.add).then_inc(x2_ready, 1)
                dve.wait_ge(x2_ready, t + 1)
                moments_of(t, t + 1)

            def top2(t):
                dve.wait_ge(logit_mm, t + 1)
                nc.vector.tensor_copy(logits[:, t, :], bank[6 + t % 2][:, D:D + E]).then_inc(logit_read, 1)
                dve.wait_ge(logit_read, t + 1)
                step(nc.vector.max(top_v[:, t, :], logits[:, t, :]))
                settle()
                step(nc.vector.max_index(top_i[:, t, :], top_v[:, t, :], logits[:, t, :]))

            row_max(0, 0)
            row_max(0, 1)
            inverse(0, 0)
            row_max(1, 0)
            inverse(0, 1)
            row_max(1, 1)
            inverse(1, 0)
            for t in range(TILES):
                if t + 2 < TILES:
                    row_max(t + 2, 0)
                if t + 1 < TILES:
                    inverse(t + 1, 1)
                if t >= 1:
                    normalise(4 + t - 1, t - 1, t)
                evac_pt(t, 0)
                evac_pt(t, 1)
                if t + 2 < TILES:
                    row_max(t + 2, 1)
                    inverse(t + 2, 0)
                evac_pt(t, 2)
                if t >= 2:
                    top2(t - 2)
                residual2(t)
            normalise(4 + TILES - 1, TILES - 1, TILES)
            top2(TILES - 2)
            top2(TILES - 1)
            settle()
            nc.vector.tensor_tensor(gap[:], top_v[:, :, 1], top_v[:, :, 0], ALU.subtract).then_inc(gap_ready, 1)
            ids = expert_ids[:].unsqueeze(2).broadcast_to([P, E, TILES])
            dve.wait_ge(consts, 5)
            for mask, place in ((mask1, 0), (mask2, 1)):
                step(nc.vector.tensor_tensor(mask[:], ids, top_i[:, :, place].unsqueeze(1).broadcast_to([P, E, TILES]),
                                             ALU.is_equal))
            dve.wait_ge(second_ready, 1)
            step(nc.vector.tensor_scalar(norm1[:], second[:], 1.0, None, ALU.add))
            settle()
            step(nc.vector.reciprocal(p1[:], norm1[:]))
            settle()
            step(nc.vector.tensor_tensor(p2[:], second[:], p1[:], ALU.mult))
            step(nc.vector.tensor_tensor(mask1[:], mask1[:], p1[:].unsqueeze(1).broadcast_to([P, E, TILES]), ALU.mult))
            settle()
            step(nc.vector.tensor_tensor(mask2[:], mask2[:], p2[:].unsqueeze(1).broadcast_to([P, E, TILES]), ALU.mult))
            settle()
            nc.vector.tensor_tensor(w_tok[:], mask1[:], mask2[:], ALU.add).then_inc(w_tok_ready, 1)
            dve.wait_ge(w_mm, 1)
            nc.vector.tensor_copy(w_rows[:], bank[4][0:E * TILES, 0:P]).then_inc(w_rows_ready, 1)

            def gated_up(u, k):
                dve.wait_ge(sil_ready, u + 1)
                dve.wait_ge(h2_mm, u + 1)
                nc.vector.tensor_tensor(prod[:, k % 2, :], sil[:, k % 2, :], bank[2 + k % 2][:],
                                        ALU.mult).then_inc(prod_ready, 1)

            for u in range(UPE):
                if u >= 2:
                    dve.wait_ge(hid_ready, u - 1)
                gated_up(u, u)
            with dve.Fori(0, E // 2) as i:
                for k in range(2 * UPE):
                    u = 8 * i + (UPE + k)
                    dve.wait_ge(hid_ready, u - 1)
                    gated_up(u, k)
            for b in range(BATCH):
                tiles = slice(b * TPB, (b + 1) * TPB)
                dve.wait_ge(fin_mm, b + 1)
                nc.vector.tensor_tensor(out_tok[:, tiles, :], x_tok[:, tiles, :],
                                        bank[4 + b][:].rearrange("p (t d) -> p t d", d=D), ALU.add).then_inc(out_ready, 1)

        @block.tensor
        def _(pe):
            pe.wait_ge(consts, 5)

            def turn(dst, src, n=P):
                return nc.tensor.transpose(dst, src, ident[0:n, 0:n])

            def prep_wait(r):
                if r >= 2:
                    pe.wait_ge(prep_evac, r - 1)

            pe.wait_ge(ctx_in_s, 48)
            for c, (r0, n) in enumerate(CTX_CUTS):
                ins = turn(bank[0][0:CTX, r0:r0 + n], ctx_rows[0:n, c, :], n)
            ins.then_inc(prep_mm, 1)
            pe.wait_ge(wqk_in, 32)
            for c in range(4):
                ins = turn(bank[1][:, c * P:(c + 1) * P], wq[:, c * P:(c + 1) * P])
            ins.then_inc(prep_mm, 1)

            def project_ctx(r, w, c):
                prep_wait(r)
                nc.tensor.matmul(bank[r % 2][:, 0:CTX_ROWS], w[:, c * P:(c + 1) * P], ctxT[:],
                                 start=True, stop=True).then_inc(prep_mm, 1)

            def merge(r, w, kv, h):
                prep_wait(r)
                rows = slice((h % 2) * DH, (h % 2 + 1) * DH)
                nc.tensor.matmul(bank[r % 2][:, 0:CTX_ROWS], w[rows, h // 2, :], kv[rows, h // 2, :],
                                 start=True, stop=True).then_inc(prep_mm, 1)

            def turn_tiles(n, b):
                pe.wait_ge(xn_ready, n + 1)
                for t in range(TPB):
                    ins = turn(bank[4 + b][:, t * P:(t + 1) * P], xn[:, b * TPB + t, :])
                ins.then_inc(xt_mm, 1)

            def gate_inputs(b):
                cols = slice(b * SEQ, (b + 1) * SEQ)
                pe.wait_ge(wzh_in, 16 * 8)
                pe.wait_ge(xt_evac, b + 1)
                if b:
                    pe.wait_ge(z_ready, b)
                nc.tensor.matmul(bank[6][:], wz[:], xnT[:, cols], start=True, stop=True).then_inc(z_mm, 1)
                if b:
                    pe.wait_ge(scan_ready, b)
                nc.tensor.matmul(bank[7][:], wh[:], xnT[:, cols], start=True, stop=True).then_inc(hh_mm, 1)

            def out_gate(b):
                pe.wait_ge(wg_in, 32)
                pe.wait_ge(scan_ready, b + 1)
                if b:
                    pe.wait_ge(gate_ready, b)
                nc.tensor.matmul(bank[2][:], wg[:], hT[:, b * SEQ:(b + 1) * SEQ],
                                 start=True, stop=True).then_inc(gate_mm, 1)

            def turn_y(b):
                pe.wait_ge(y_ready, b + 1)
                if b:
                    pe.wait_ge(x1_ready, b)
                for t in range(TPB):
                    ins = turn(bank[3][:, t * P:(t + 1) * P], yT[:, b * SEQ + t * P:b * SEQ + (t + 1) * P])
                ins.then_inc(ytok_mm, 1)

            def turn_u(b, g):
                r = 26 + 3 * b + g
                prep_wait(r)
                if r == 26:
                    pe.wait_ge(prep_evac, 26)
                c0, n = GROUPS[g]
                flat = UT[:, b, :, :].rearrange("p h l -> p (h l)")
                for c in range(c0, c0 + n):
                    m = rows_of(c)
                    ins = turn(bank[r % 2][0:m, (c - c0) * P:(c - c0) * P + P], flat[:, c * P:c * P + m])
                ins.then_inc(prep_mm, 1)

            for c in range(4):
                if c == 0:
                    pe.wait_ge(prep_evac, 1)
                project_ctx(2 + c, wk, c)
            turn_tiles(0, 0)
            gate_inputs(0)
            pe.wait_ge(wvo_in, 32)
            for c in range(4):
                project_ctx(6 + c, wv, c)
            turn_tiles(1, 1)
            gate_inputs(1)
            for h in range(4):
                merge(10 + h, wqT, kT, h)
            out_gate(0)
            for h in range(4, 8):
                merge(10 + h, wqT, kT, h)
            turn_y(0)
            out_gate(1)
            for h in range(8):
                if h == 4:
                    turn_y(1)
                merge(18 + h, wo, vT, h)
            for b in range(BATCH):
                turn_tiles(2 + b, b)
                for g in range(3):
                    turn_u(b, g)

            def scores(t, hh):
                s = 2 * t + hh
                if t >= 1:
                    pe.wait_ge(exp_done, s - 1)
                elif hh == 0:
                    pe.wait_ge(prep_evac, 32)
                    pe.wait_ge(gate_ready, 2)
                    pe.wait_ge(x1_ready, 2)
                if t % TPB == 0 and hh == 0:
                    pe.wait_ge(xt_evac, 3 + t // TPB)
                for j in range(2):
                    h0 = hh * HPU + 2 * j
                    ins = nc.tensor.matmul(bank[2 * hh + j][:, 0:2 * CL], xnT[:, t * P:(t + 1) * P],
                                           A[:, t // TPB, h0:h0 + 2, :].rearrange("p h l -> p (h l)"),
                                           start=True, stop=True)
                ins.then_inc(s_mm, 1)

            def turn_probs(t, g):
                pe.wait_ge(pn_ready, 2 * t + 2)
                if g == 0 and t >= 2:
                    pe.wait_ge(xt3_evac, t - 1)
                if g == 1 and t >= 1:
                    pe.wait_ge(pt_evac, 3 * t)
                if g == 2:
                    pe.wait_ge(pt_evac, 3 * t + 2)
                c0, n = GROUPS[g]
                flat = probs[:, t % 3, :, :].rearrange("p h l -> p (h l)")
                for c in range(c0, c0 + n):
                    m = rows_of(c)
                    ins = turn(bank[4 if g == 0 else 5][0:m, (c - c0) * P:(c - c0) * P + P],
                               flat[:, c * P:c * P + m])
                ins.then_inc(pt_mm, 1)

            def turn_tile3(t):
                pe.wait_ge(xn_ready, 4 + t + 1)
                if t + 1 < TILES:
                    pe.wait_ge(pt_evac, 3 * (t + 1) + 1)
                turn(bank[4][:, 0:P], xn[:, t, :]).then_inc(xt3_mm, 1)

            def attend(t):
                if t >= 1:
                    pe.wait_ge(x2_ready, t)
                if t >= 2:
                    pe.wait_ge(logit_read, t - 1)
                for c in range(NCH):
                    m = rows_of(c)
                    if c in (0, 4, 8):
                        pe.wait_ge(pt_evac, 3 * t + c // 4 + 1)
                    ins = nc.tensor.matmul(bank[6 + t % 2][:, 0:D], probsT[0:m, t % 2, c, :],
                                           U[0:m, t // TPB, c, :], start=(c == 0), stop=(c == NCH - 1))
                ins.then_inc(pv_mm, 1)

            def route(t):
                if t == 0:
                    pe.wait_ge(gw_in, 16)
                pe.wait_ge(xt3_evac, t + 1)
                pe.wait_ge(x2_ready, t + 1)
                nc.tensor.matmul(bank[6 + t % 2][:, D:D + E], xnT[:, t * P:(t + 1) * P], gate_w[:],
                                 start=True, stop=True).then_inc(logit_mm, 1)

            for s in range(4):
                scores(s // 2, s % 2)
            for t in range(TILES):
                if t + 2 < TILES:
                    scores(t + 2, 0)
                turn_probs(t, 0)
                turn_probs(t, 1)
                if t >= 1:
                    turn_tile3(t - 1)
                if t + 2 < TILES:
                    scores(t + 2, 1)
                turn_probs(t, 2)
                if t >= 1:
                    route(t - 1)
                attend(t)
            turn_tile3(TILES - 1)
            route(TILES - 1)

            def up(u, k, par):
                n, c = k % UPE // HC, k % HC
                cols = slice(n * SEQ, (n + 1) * SEQ)
                nc.tensor.matmul(bank[k % 2][:], w1s[par][:, c * P:(c + 1) * P], xnT[:, cols],
                                 start=True, stop=True).then_inc(h1_mm, 1)
                nc.tensor.matmul(bank[2 + k % 2][:], w2s[par][:, c * P:(c + 1) * P], xnT[:, cols],
                                 start=True, stop=True).then_inc(h2_mm, 1)

            def down(u, k, par, last=False):
                n, c = k % UPE // HC, k % HC
                pe.wait_ge(hid_ready, u + 1)
                nc.tensor.matmul(bank[6 + n][:], w3s[par][:, c, :], hidden[:, k % UPE, :],
                                 start=False, stop=last and c == HC - 1,
                                 skip_group_check=True).then_inc(o_mm, 1)

            pe.wait_ge(ew_in[1], 48)
            pe.wait_ge(xt3_evac, TILES)
            pe.wait_ge(exp_done, 2 * TILES)
            pe.wait_ge(logit_read, TILES)
            for n in range(BATCH):
                nc.tensor.matmul(bank[6 + n][:], zeros[:, 0:P], zeros[:], start=True, stop=False,
                                 skip_group_check=True)
            for u in range(UPE):
                if u == 2:
                    pe.wait_ge(w_tok_ready, 1)
                    turn(bank[4][0:E * TILES, 0:P], w_tok[:].rearrange("p e t -> p (e t)")).then_inc(w_mm, 1)
                if u >= 2:
                    pe.wait_ge(sil_ready, u - 1)
                    pe.wait_ge(prod_ready, u - 1)
                up(u, u, 1)
                if u >= 2:
                    down(u - 2, u - 2, 1)
            with pe.Fori(0, E // 2) as i:
                for k in range(2 * UPE):
                    u = 8 * i + (UPE + k)
                    par = k // UPE
                    if k % UPE == 0:
                        pe.wait_ge(ew_in[par], 48 * i + 48 * (1 + par))
                    pe.wait_ge(sil_ready, u - 1)
                    pe.wait_ge(prod_ready, u - 1)
                    up(u, k, par)
                    if k >= 2:
                        down(u - 2, k - 2, (k - 2) // UPE, last=False)
                    else:
                        down(u - 2, k + 2, 1)
            last = (E + 1) * UPE
            down(last - 2, 2, 1, last=True)
            down(last - 1, 3, 1, last=True)
            pe.wait_ge(w_rows_ready, 1)
            for b in range(BATCH):
                pe.wait_ge(moe_evac, b + 1)
                for t in range(TPB):
                    ins = turn(bank[4 + b][:, t * P:(t + 1) * P], moeT[:, b * SEQ + t * P:b * SEQ + (t + 1) * P])
                ins.then_inc(fin_mm, 1)


_INS = ["x", "ctx_768", "L0_attn_W_zf", "L0_attn_b_zf", "L0_attn_W_hf", "L0_attn_b_hf", "L0_attn_W_zs",
        "L0_attn_b_zs", "L0_attn_W_hs", "L0_attn_b_hs", "L0_attn_W_g", "L0_attn_b_g", "L0_xattn_Wq",
        "L0_xattn_Wk", "L0_xattn_Wv", "L0_xattn_Wo", "L0_xattn_bo", "L0_ffn_gate_w", "L0_ffn_ew1",
        "L0_ffn_ew2", "L0_ffn_ew3", "L0_ffn_sw1", "L0_ffn_sw2", "L0_ffn_sw3"]


def kernel(**inputs):
    import numpy as _np
    import concourse.bacc as _bacc
    from concourse import mybir as _mybir
    from concourse.bass_utils import run_bass_kernel_spmd as _run

    nc = _bacc.Bacc("TRN2", target_bir_lowering=False, num_devices=1)
    arrays, args = {}, []
    for name in _INS:
        a = _np.ascontiguousarray(inputs[name])
        arrays[f"in_{name}"] = a
        args.append(nc.dram_tensor(f"in_{name}", a.shape, _mybir.dt.from_np(a.dtype), kind="ExternalInput").ap())
    args.append(nc.dram_tensor("router_scratch", (8, 1024), _mybir.dt.float32).ap())
    args.append(nc.dram_tensor("out_0", (2, 512, 128), _mybir.dt.float32, kind="ExternalOutput").ap())
    decoder_block(nc, *args)
    return _run(nc, [arrays], core_ids=[0]).results[0]["out_0"]
```

```python
import math
from contextlib import ExitStack

import concourse.bass as bass
from concourse import mybir

F32 = mybir.dt.float32
F32R = mybir.dt.float32r
BF16 = mybir.dt.bfloat16
U32 = mybir.dt.uint32
ALU = mybir.AluOpType
ACT = mybir.ActivationFunctionType
AX_X = mybir.AxisListType.X

P = 128
D = 128
BATCH, SEQ = 2, 512
TOK = BATCH * SEQ
TILES = TOK // P
TPB = SEQ // P
CH = 64
CTX, CL = 96, 154
CTX_ROWS = BATCH * CL
HEADS, DH = 8, 64
INNER = HEADS * DH
HL = HEADS * CL
NCH = (HL + P - 1) // P
HPU = 4
E, H = 8, 256
HC = H // P
UPE = BATCH * HC
UNITS = (E + 1) * UPE
EPS = 1e-5
CTX_CUT = 4
CTX_TILE = CTX_ROWS // CTX_CUT
GROUPS = [(0, 4), (4, 4), (8, NCH - 8)]


def rows_of(c):
    return min(P, HL - c * P)


def f32(ap):
    return ap.bitcast(F32)


def split_product(nc, dst, lhs, rhs, start=True, stop=True, **kw):
    nc.tensor.matmul(dst, lhs[0], rhs[0], start=start, stop=False, **kw)
    nc.tensor.matmul(dst, lhs[0], rhs[1], start=False, stop=False, **kw)
    return nc.tensor.matmul(dst, lhs[1], rhs[0], start=False, stop=stop, **kw)


def decoder_block(nc, x, ctx_in, w_zf, b_zf, w_hf, b_hf, w_zs, b_zs, w_hs, b_hs, w_g, b_g,
                  w_q, w_k, w_v, w_o, b_o, w_gate, ew1, ew2, ew3, sw1, sw2, sw3, scratch, out):
    with ExitStack() as ctx:
        def sb(name, shape, dt=F32):
            return ctx.enter_context(nc.sbuf_tensor(name, shape, dt))

        def sem(name):
            return ctx.enter_context(nc.semaphore(name))

        bank = [ctx.enter_context(nc.psum_tensor(f"bank{i}", [P, 512], F32)) for i in range(8)]

        ident = sb("ident", [P, P])
        minus_half = sb("minus_half", [P, TILES])
        euler = sb("euler", [P, TILES])
        zeros = sb("zeros", [1, 512], BF16)
        expert_ids = sb("expert_ids", [P, E])
        x_tok = sb("x_tok", [P, TILES, D])
        xn = sb("xn", [P, TILES, D])
        stats = sb("stats", [P, TILES, 6])
        moments = sb("moments", [P, TILES, 2])
        var_eps = sb("var_eps", [P, TILES])
        rstd = sb("rstd", [P, TILES])
        xnT = sb("xnT", [P, TOK])
        x_hi, x_lo = sb("x_hi", [P, TOK], F32R), sb("x_lo", [P, TOK], F32R)
        wz, wh, wg = sb("wz", [P, P]), sb("wh", [P, P]), sb("wg", [P, P])
        bz, bh, bg = sb("bz", [P, 1]), sb("bh", [P, 1]), sb("bg", [P, 1])
        zT, decayT, driveT = sb("zT", [P, TOK]), sb("decayT", [P, TOK]), sb("driveT", [P, TOK])
        hT, gateT, yT = sb("hT", [P, TOK]), sb("gateT", [P, TOK]), sb("yT", [P, TOK])
        ctx_rows = sb("ctx_rows", [CTX_TILE, CTX_CUT, CTX])
        ctxT_hi, ctxT_lo = sb("ctxT_hi", [CTX, CTX_ROWS], F32R), sb("ctxT_lo", [CTX, CTX_ROWS], F32R)
        wq, wk, wv = sb("wq", [P, INNER]), sb("wk", [CTX, INNER]), sb("wv", [CTX, INNER])
        wk_hi, wk_lo = sb("wk_hi", [CTX, INNER], F32R), sb("wk_lo", [CTX, INNER], F32R)
        wv_hi, wv_lo = sb("wv_hi", [CTX, INNER], F32R), sb("wv_lo", [CTX, INNER], F32R)
        wo = sb("wo", [P, 4, D])
        wqT = sb("wqT", [P, 4, D])
        kT, vT = sb("kT", [P, 4, CTX_ROWS]), sb("vT", [P, 4, CTX_ROWS])
        A_hi, A_lo = sb("A_hi", [P, BATCH, HEADS, CL], F32R), sb("A_lo", [P, BATCH, HEADS, CL], F32R)
        UT = sb("UT", [P, BATCH, HEADS, CL])
        U = sb("U", [P, BATCH, NCH, D])
        bo_rows = sb("bo_rows", [P, D])
        probs = sb("probs", [P, 3, HEADS, CL])
        neg_max = sb("neg_max", [P, 2 * TILES, HPU])
        row_sum = sb("row_sum", [P, 2 * TILES, HPU])
        inv_sum = sb("inv_sum", [P, 2 * TILES, HPU])
        probsT = sb("probsT", [P, 2, NCH, P])
        gate_w = sb("gate_w", [P, E])
        gw_hi, gw_lo = sb("gw_hi", [P, E], F32R), sb("gw_lo", [P, E], F32R)
        logits = sb("logits", [P, TILES, E])
        top_v = sb("top_v", [P, TILES, 8])
        top_i = sb("top_i", [P, TILES, 8], U32)
        gap = sb("gap", [P, TILES])
        second = sb("second", [P, TILES])
        norm1, p1, p2 = sb("norm1", [P, TILES]), sb("p1", [P, TILES]), sb("p2", [P, TILES])
        mask1, mask2 = sb("mask1", [P, E, TILES]), sb("mask2", [P, E, TILES])
        w_tok = sb("w_tok", [P, E, TILES])
        w_rows = sb("w_rows", [E * TILES, P])
        share = [sb(f"share{p}", [P, TOK]) for p in range(2)]
        w_raw = [sb(f"w_raw{p}", [P, 3 * H]) for p in range(2)]
        w_hi = [sb(f"w_hi{p}", [P, 3 * H], F32R) for p in range(2)]
        w_lo = [sb(f"w_lo{p}", [P, 3 * H], F32R) for p in range(2)]
        sil, prod = sb("sil", [P, 2, 512]), sb("prod", [P, 2, 512])
        hidden = sb("hidden", [P, 2, 512])
        hid_hi, hid_lo = sb("hid_hi", [P, UPE, 512], F32R), sb("hid_lo", [P, UPE, 512], F32R)
        moeT = sb("moeT", [P, TOK])

        z_bank, h_bank = (bank[6], bank[4]), (bank[7], bank[5])

        x_in = [sem(f"x_in{b}") for b in range(BATCH)]
        wzh_in, wg_in, bias_in, ctx_in_s, bo_in, gw_in = (
            sem(n) for n in ("wzh_in", "wg_in", "bias_in", "ctx_in", "bo_in", "gw_in"))
        wk_in, wv_in, wq_in, wo_in = (sem(n) for n in ("wk_in", "wv_in", "wq_in", "wo_in"))
        consts = sem("consts")
        dve_step = sem("dve_step")
        var_ready, rstd_ready, xn_ready = sem("var_ready"), sem("rstd_ready"), sem("xn_ready")
        xt_mm, xt_evac = sem("xt_mm"), sem("xt_evac")
        z_mm, hh_mm, z_ready, scan_ready = (sem(n) for n in ("z_mm", "hh_mm", "z_ready", "scan_ready"))
        gate_mm, gate_ready, y_ready, ytok_mm, x1_ready = (
            sem(n) for n in ("gate_mm", "gate_ready", "y_ready", "ytok_mm", "x1_ready"))
        prep_mm, prep_evac, prep_lo = sem("prep_mm"), sem("prep_evac"), sem("prep_lo")
        wkv_hi, wkv_lo, gw_split, first_hi, first_lo = (
            sem(n) for n in ("wkv_hi", "wkv_lo", "gw_split", "first_hi", "first_lo"))
        u_mm, u_evac, x_lo_ready, bo_added, w_split_hi, w_split_lo = (
            sem(n) for n in ("u_mm", "u_evac", "x_lo_ready", "bo_added", "w_split_hi", "w_split_lo"))
        ones_ready = sem("ones_ready")
        hi_ready, lo_ready = sem("hi_ready"), sem("lo_ready")
        s_mm, max_ready, exp_done, inv_ready, pn_ready = (
            sem(n) for n in ("s_mm", "max_ready", "exp_done", "inv_ready", "pn_ready"))
        pt_mm, pt0_evac, pt_evac, pv_mm, x2_ready = (
            sem(n) for n in ("pt_mm", "pt0_evac", "pt_evac", "pv_mm", "x2_ready"))
        xt3_mm, xt3_hi, xt3_lo = (sem(n) for n in ("xt3_mm", "xt3_hi", "xt3_lo"))
        logit_mm, logit_read, gap_ready, second_ready = (
            sem(n) for n in ("logit_mm", "logit_read", "gap_ready", "second_ready"))
        w_tok_ready, w_mm, w_rows_ready, w_stored = (
            sem(n) for n in ("w_tok_ready", "w_mm", "w_rows_ready", "w_stored"))
        share_in = [sem(f"share_in{p}") for p in range(2)]
        ew_in = [sem(f"ew_in{p}") for p in range(2)]
        h1_mm, h2_mm, o_mm, sil_ready, prod_ready, hid_ready = (
            sem(n) for n in ("h1_mm", "h2_mm", "o_mm", "sil_ready", "prod_ready", "hid_ready"))
        moe_evac, fin_mm, out_ready, stored = (
            sem(n) for n in ("moe_evac", "fin_mm", "out_ready", "stored"))

        x_view = x.rearrange("b (t p) d -> b p t d", p=P)
        out_view = out.rearrange("b (t p) d -> b p t d", p=P)
        col = lambda v: v.rearrange("(n a) -> n a", a=1)
        row = lambda v: v.rearrange("(a n) -> a n", a=1)

        block = ctx.enter_context(nc.Block())

        @block.sync
        def _(sp):
            def load_expert(p, a1, a2, a3):
                sp.dma_start(w_raw[p][:, 0:H], a1).then_inc(ew_in[p], 16)
                sp.dma_start(w_raw[p][:, H:2 * H], a2).then_inc(ew_in[p], 16)
                sp.dma_start(w_raw[p][:, 2 * H:3 * H].rearrange("p (c n) -> p c n", c=HC),
                             a3.rearrange("(c p) n -> p c n", p=P)).then_inc(ew_in[p], 16)

            def load_share(p, e):
                sp.dma_start(share[p][:], scratch[bass.ds(e, 1), :].broadcast_to([P, TOK])).then_inc(share_in[p], 16)

            for b in range(BATCH):
                sp.dma_start(x_tok[:, b * TPB:(b + 1) * TPB, :], x_view[b]).then_inc(x_in[b], 16)
            sp.dma_start(wz[:, 0:CH], w_zf).then_inc(wzh_in, 16)
            sp.dma_start(wz[:, CH:P], w_zs).then_inc(wzh_in, 16)
            sp.dma_start(wh[:, 0:CH], w_hf).then_inc(wzh_in, 16)
            sp.dma_start(wh[:, CH:P], w_hs).then_inc(wzh_in, 16)
            sp.dma_start(bz[0:CH, :], col(b_zf)).then_inc(bias_in, 16)
            sp.dma_start(bz[CH:P, :], col(b_zs)).then_inc(bias_in, 16)
            sp.dma_start(bh[0:CH, :], col(b_hf)).then_inc(bias_in, 16)
            sp.dma_start(bh[CH:P, :], col(b_hs)).then_inc(bias_in, 16)
            sp.dma_start(bg[:], col(b_g)).then_inc(bias_in, 16)
            sp.dma_start(wg[:], w_g).then_inc(wg_in, 16)
            sp.dma_start(wq[:], w_q).then_inc(wq_in, 16)
            sp.dma_start(wo[:], w_o.rearrange("(c p) n -> p c n", p=P)).then_inc(wo_in, 16)
            sp.dma_start(gate_w[:], w_gate).then_inc(gw_in, 16)
            load_expert(0, sw1, sw2, sw3)
            load_expert(1, ew1[0], ew2[0], ew3[0])
            sp.dma_start(bo_rows[:], row(b_o).broadcast_to([P, D])).then_inc(bo_in, 16)
            for n in (2, 3):
                sp.wait_ge(first_lo, n - 1)
                load_expert(n % 2, ew1[n - 1], ew2[n - 1], ew3[n - 1])
            sp.wait_ge(w_rows_ready, 1)
            sp.dma_start(scratch.rearrange("e (t p) -> (e t) p", p=P), w_rows[:]).then_inc(w_stored, 16)
            sp.wait_ge(w_stored, 16)
            load_share(1, 0)
            sp.wait_ge(hid_ready, UPE)
            load_share(0, 1)

            with sp.Fori(0, 2) as i:
                for j in range(2):
                    n = 2 * i + (4 + j)
                    sp.wait_ge(w_split_lo, 6 * i + (3 + 3 * j))
                    load_expert(j, ew1[n - 1], ew2[n - 1], ew3[n - 1])
                    sp.wait_ge(hid_ready, 8 * i + (8 + 4 * j))
                    load_share(1 - j, n - 2)
            sp.wait_ge(w_split_lo, 15)
            load_expert(0, ew1[E - 1], ew2[E - 1], ew3[E - 1])
            for n in (E - 1, E):
                sp.wait_ge(hid_ready, UPE * (n - 1))
                load_share(n % 2, n - 1)
            for b in range(BATCH):
                sp.wait_ge(out_ready, b + 1)
                sp.dma_start(out_view[b], x_tok[:, b * TPB:(b + 1) * TPB, :]).then_inc(stored, 16)
            sp.wait_ge(stored, 16 * BATCH)

        @block.gpsimd
        def _(pool):
            nc.gpsimd.memset(ident[:], 0.0).then_inc(consts, 1)
            nc.gpsimd.memset(minus_half[:], -0.5).then_inc(consts, 1)
            nc.gpsimd.memset(euler[:], math.e).then_inc(consts, 1)
            nc.gpsimd.iota(expert_ids[:], pattern=[[1, E]], base=0, channel_multiplier=0,
                           allow_small_or_imprecise_dtypes=True).then_inc(consts, 1)
            nc.gpsimd.memset(zeros[:], 0.0).then_inc(consts, 1)
            pool.wait_ge(consts, 5)
            nc.gpsimd.affine_select(out=ident[:], in_=ident[:], compare_op=ALU.not_equal, fill=1.0,
                                    base=0, pattern=[[-1, P]], channel_multiplier=1).then_inc(consts, 1)
            pool.wait_ge(consts, 6)

            def rsqrt(n, t0, t1):
                pool.wait_ge(var_ready, n + 1)
                nc.gpsimd.tensor_tensor(rstd[:, t0:t1], var_eps[:, t0:t1], minus_half[:, t0:t1],
                                        ALU.pow).then_inc(rstd_ready, 1)

            def low_half(n, dst, src, hi):
                pool.wait_ge(wkv_hi, n + 1)
                nc.gpsimd.tensor_tensor(dst, src, f32(hi), ALU.subtract).then_inc(wkv_lo, 1)

            rsqrt(0, 0, TPB)
            low_half(0, wk_lo[:], wk[:], wk_hi[:])
            rsqrt(1, TPB, TILES)
            low_half(1, wv_lo[:], wv[:], wv_hi[:])
            pool.wait_ge(gw_in, 16)
            nc.gpsimd.tensor_copy(gw_hi[:], gate_w[:]).then_inc(gw_split, 1)
            pool.wait_ge(gw_split, 1)
            nc.gpsimd.tensor_tensor(gw_lo[:], gate_w[:], f32(gw_hi[:]), ALU.subtract).then_inc(gw_split, 1)
            nc.gpsimd.memset(share[0][:], 1.0).then_inc(ones_ready, 1)

            def split_first(p):
                pool.wait_ge(ew_in[p], 48)
                nc.gpsimd.tensor_copy(w_hi[p][:], w_raw[p][:]).then_inc(first_hi, 1)
                pool.wait_ge(first_hi, p + 1)
                nc.gpsimd.tensor_tensor(w_lo[p][:], w_raw[p][:], f32(w_hi[p][:]), ALU.subtract).then_inc(first_lo, 1)

            split_first(0)
            rsqrt(2, 0, TPB)
            rsqrt(3, TPB, TILES)
            split_first(1)

            def normalise(t, hh):
                s = 2 * t + hh
                pool.wait_ge(inv_ready, s + 1)
                view = probs[:, t % 3, hh * HPU:(hh + 1) * HPU, :]
                nc.gpsimd.tensor_tensor(view, view, inv_sum[:, s, :].unsqueeze(2).broadcast_to([P, HPU, CL]),
                                        ALU.mult).then_inc(pn_ready, 1)

            normalise(0, 0)
            pool.wait_ge(bo_in, 16)
            pool.wait_ge(xn_ready, 4)
            nc.gpsimd.tensor_tensor(x_tok[:], x_tok[:], bo_rows[:].unsqueeze(1).broadcast_to([P, TILES, D]),
                                    ALU.add).then_inc(bo_added, 1)
            normalise(0, 1)
            normalise(1, 0)
            for t in range(TILES + 2):
                if t >= 2:
                    rsqrt(2 * BATCH + t - 2, t - 2, t - 1)
                if t + 1 < TILES:
                    normalise(t + 1, 1)
                if t + 2 < TILES:
                    normalise(t + 2, 0)

            def weigh(u, k, par, least):
                n = k // HC
                pool.wait_ge(prod_ready, u + 1)
                if least >= 2:
                    pool.wait_ge(lo_ready, u - 1)
                nc.gpsimd.tensor_tensor(hidden[:, k % 2, :], prod[:, k % 2, :],
                                        share[par][:, n * SEQ:(n + 1) * SEQ], ALU.mult).then_inc(hid_ready, 1)

            pool.wait_ge(gap_ready, 1)
            nc.gpsimd.tensor_tensor(second[:], euler[:], gap[:], ALU.pow).then_inc(second_ready, 1)
            pool.wait_ge(ones_ready, 1)
            for k in range(UPE):
                weigh(k, k, 0, k)
            with pool.Fori(0, E // 2) as i:
                for par in (1, 0):
                    pool.wait_ge(share_in[par], 16 * i + 16)
                    for k in range(UPE):
                        weigh(8 * i + (UPE * (2 - par) + k), k, par, UPE)

        @block.scalar
        def _(act):
            act.dma_start(ctx_rows[:], ctx_in.rearrange("b l c -> (b l) c").rearrange("(c p) n -> p c n", p=CTX_TILE)
                          ).then_inc(ctx_in_s, 16)
            act.dma_start(wk[:], w_k).then_inc(wk_in, 16)
            act.preload_act_table(ACT.Sigmoid)
            act.dma_start(wv[:], w_v).then_inc(wv_in, 16)

            def copy(dst, src, scale=1.0):
                return nc.scalar.activation(dst, src, ACT.Copy, scale=scale)

            def prep(r, dst, src, scale=1.0):
                act.wait_ge(prep_mm, r + 1)
                copy(dst, src, scale).then_inc(prep_evac, 1)

            def prep_kv(r, kv):
                prep(r, kv[:, (r - 1) % 4, :], bank[r % 4][:, 0:CTX_ROWS])

            def prep_merged(r, dst):
                prep(r, dst[:, :, (r - 10) % HEADS, :],
                     bank[r % 4][:, 0:CTX_ROWS].rearrange("p (b l) -> p b l", b=BATCH))

            def forget_gate(b):
                act.wait_ge(z_mm, b + 1)
                nc.scalar.activation(zT[:, b * SEQ:(b + 1) * SEQ], z_bank[b][:], ACT.Sigmoid,
                                     bias=bz[:, 0:1]).then_inc(z_ready, 1)

            def out_gate(b):
                act.wait_ge(gate_mm, b + 1)
                nc.scalar.activation(gateT[:, b * SEQ:(b + 1) * SEQ], z_bank[b][:], ACT.Sigmoid,
                                     bias=bg[:, 0:1]).then_inc(gate_ready, 1)

            def evac_xt(n, b, dst):
                act.wait_ge(xt_mm, n + 1)
                src = bank[4 + b] if n < 2 else z_bank[b]
                copy(dst[:, b * SEQ:(b + 1) * SEQ], src[:]).then_inc(xt_evac, 1)

            act.wait_ge(wk_in, 16)
            copy(wk_hi[:], wk[:]).then_inc(wkv_hi, 1)
            prep(0, ctxT_hi[:], bank[0][0:CTX, 0:CTX_ROWS])
            evac_xt(0, 0, xnT)
            prep_kv(1, kT)
            evac_xt(1, 1, xnT)
            act.wait_ge(wv_in, 16)
            copy(wv_hi[:], wv[:]).then_inc(wkv_hi, 1)
            act.wait_ge(bias_in, 80)
            forget_gate(0)
            prep_kv(2, kT)
            forget_gate(1)
            prep_kv(3, kT)
            prep_kv(4, kT)
            out_gate(0)
            prep_kv(5, vT)
            prep_kv(6, vT)
            out_gate(1)
            act.preload_act_table(ACT.Exp)
            prep_kv(7, vT)
            prep_kv(8, vT)
            prep(9, wqT[:].rearrange("p c d -> p (c d)"), bank[1][:], scale=DH ** -0.5)
            for r in range(10, 18):
                prep_merged(r, A_hi)
            evac_xt(2, 0, x_hi)
            for r in range(18, 26):
                prep_merged(r, UT)

            def exps(t, hh):
                s = 2 * t + hh
                act.wait_ge(max_ready, s + 1)
                if t >= 3:
                    act.wait_ge(pt_mm, 3 * (t - 2))
                for q in range(HPU):
                    ins = nc.scalar.activation(probs[:, t % 3, hh * HPU + q, :],
                                               bank[2 * hh + q // 2][:, (q % 2) * CL:(q % 2 + 1) * CL], ACT.Exp,
                                               bias=neg_max[:, s, q:q + 1], accum_out=row_sum[:, s, q:q + 1])
                ins.then_inc(exp_done, 1)

            def evac_u(b):
                for g, (c0, n) in enumerate(GROUPS):
                    act.wait_ge(u_mm, 3 * b + g + 1)
                    src = h_bank[(3 * b + g) % 2]
                    if g < 2:
                        copy(U[:, b, c0:c0 + n, :], src[:].rearrange("p (c d) -> p c d", d=D)).then_inc(u_evac, 1)
                    else:
                        copy(U[:, b, 8, :], src[:, 0:D])
                        copy(U[0:rows_of(9), b, 9, :], src[0:rows_of(9), D:2 * D]).then_inc(u_evac, 1)

            def evac_pt(t):
                act.wait_ge(pt_mm, 3 * t + 1)
                if t >= 2:
                    act.wait_ge(pv_mm, t - 1)
                copy(probsT[:, t % 2, 0:4, :], bank[4][:].rearrange("p (c d) -> p c d", d=P)).then_inc(pt0_evac, 1)

            exps(0, 0)
            exps(0, 1)
            evac_u(0)
            evac_xt(3, 1, x_hi)
            exps(1, 0)
            evac_u(1)
            exps(1, 1)
            for t in range(TILES):
                evac_pt(t)
                if t + 2 < TILES:
                    exps(t + 2, 0)
                    exps(t + 2, 1)
            act.preload_act_table(ACT.Silu)

            def silu(u, k, least):
                act.wait_ge(h1_mm, u + 1)
                if least >= 2:
                    act.wait_ge(prod_ready, u - 1)
                nc.scalar.activation(sil[:, k % 2, :], bank[k % 2][:], ACT.Silu).then_inc(sil_ready, 1)

            def high_half(u, k, least):
                act.wait_ge(hid_ready, u + 1)
                if least >= 4:
                    act.wait_ge(o_mm, u - 3)
                copy(hid_hi[:, k, :], hidden[:, k % 2, :]).then_inc(hi_ready, 1)

            def split_next(n, k, par, uses):
                if k == 1:
                    act.wait_ge(ew_in[par], uses)
                    act.wait_ge(h2_mm, UPE * n)
                if k == 3:
                    act.wait_ge(o_mm, UPE * n)
                part = slice((k - 1) * H, k * H)
                copy(w_hi[par][:, part], w_raw[par][:, part]).then_inc(w_split_hi, 1)

            def stages(n, par, first, last, uses=None):
                for k in range(UPE):
                    u = UPE * n + k
                    least = k if first else UPE + k
                    silu(u, k, least)
                    if k >= 1 and not first and not last:
                        split_next(n, k, 1 - par, uses)
                    if least >= 1:
                        high_half(u - 1, (k - 1) % UPE, least - 1)

            stages(0, 0, True, False)
            with act.Fori(0, E // 2 - 1) as i:
                stages(2 * i + 1, 1, False, False, 48 * i + 96)
                stages(2 * i + 2, 0, False, False, 48 * i + 96)
            stages(E - 1, 1, False, False, 48 * (E // 2 + 1))
            stages(E, 0, False, True)

            def evac_moe(b):
                act.wait_ge(o_mm, UNITS - 2 + 2 * b)
                copy(moeT[:, b * SEQ:(b + 1) * SEQ], bank[6 + b][:]).then_inc(moe_evac, 1)

            evac_moe(0)
            high_half(UNITS - 1, UPE - 1, UNITS - 1)
            evac_moe(1)

        @block.vector
        def _(dve):
            steps = [0]

            def step(ins):
                steps[0] += 1
                ins.then_inc(dve_step, 1)

            def settle():
                dve.wait_ge(dve_step, steps[0])

            def moments_of(t0, t1):
                for t in range(t0, t1):
                    step(nc.vector.bn_stats(stats[:, t, :], x_tok[:, t, :]))
                settle()
                for t in range(t0, t1):
                    step(nc.vector.bn_aggr(moments[:, t, :], stats[:, t, :]))
                settle()
                nc.vector.tensor_scalar(var_eps[:, t0:t1], moments[:, t0:t1, 1], EPS, None,
                                        ALU.add).then_inc(var_ready, 1)

            def normalise(n, t0, t1):
                dve.wait_ge(rstd_ready, n + 1)
                for t in range(t0, t1):
                    ins = nc.vector.tensor_scalar(xn[:, t, :], x_tok[:, t, :], moments[:, t, 0:1],
                                                  rstd[:, t:t + 1], ALU.subtract, ALU.mult)
                ins.then_inc(xn_ready, 1)

            def half(b):
                return slice(b * SEQ, (b + 1) * SEQ)

            for b in range(BATCH):
                dve.wait_ge(x_in[b], 16)
                moments_of(b * TPB, (b + 1) * TPB)
            normalise(0, 0, TPB)
            dve.wait_ge(prep_evac, 1)
            nc.vector.tensor_tensor(ctxT_lo[:], bank[0][0:CTX, 0:CTX_ROWS], f32(ctxT_hi[:]),
                                    ALU.subtract).then_inc(prep_lo, 1)
            normalise(1, TPB, TILES)
            dve.wait_ge(bias_in, 80)
            for b in range(BATCH):
                dve.wait_ge(z_ready, b + 1)
                step(nc.vector.tensor_scalar(decayT[:, half(b)], zT[:, half(b)], -1.0, 1.0, ALU.mult, ALU.add))
                dve.wait_ge(hh_mm, b + 1)
                step(nc.vector.scalar_tensor_tensor(driveT[:, half(b)], h_bank[b][:], bh[:, 0:1], zT[:, half(b)],
                                                    ALU.add, ALU.mult))
                settle()
                nc.vector.tensor_tensor_scan(hT[:, half(b)], decayT[:, half(b)], driveT[:, half(b)], 0.0,
                                             ALU.mult, ALU.add).then_inc(scan_ready, 1)

            def gated(b):
                dve.wait_ge(gate_ready, b + 1)
                dve.wait_ge(scan_ready, b + 1)
                nc.vector.tensor_tensor(yT[:, half(b)], gateT[:, half(b)], hT[:, half(b)],
                                        ALU.mult).then_inc(y_ready, 1)

            def residual1(b):
                tiles = slice(b * TPB, (b + 1) * TPB)
                dve.wait_ge(ytok_mm, b + 1)
                nc.vector.tensor_tensor(x_tok[:, tiles, :], x_tok[:, tiles, :],
                                        h_bank[b][:].rearrange("p (t d) -> p t d", d=D), ALU.add).then_inc(x1_ready, 1)
                dve.wait_ge(x1_ready, b + 1)
                moments_of(b * TPB, (b + 1) * TPB)

            def low_half_a(h):
                dve.wait_ge(prep_evac, 10 + h + 1)
                nc.vector.tensor_tensor(A_lo[:, :, h, :],
                                        bank[(10 + h) % 4][:, 0:CTX_ROWS].rearrange("p (b l) -> p b l", b=BATCH),
                                        f32(A_hi[:, :, h, :]), ALU.subtract).then_inc(prep_lo, 1)

            def low_half_x(b):
                dve.wait_ge(xt_evac, 2 + b + 1)
                nc.vector.tensor_tensor(x_lo[:, half(b)], z_bank[b][:], f32(x_hi[:, half(b)]),
                                        ALU.subtract).then_inc(x_lo_ready, 1)

            gated(0)
            gated(1)
            residual1(0)
            normalise(2, 0, TPB)
            residual1(1)
            normalise(3, TPB, TILES)
            for h in range(HEADS):
                low_half_a(h)
            low_half_x(0)

            def row_max(t, hh):
                s = 2 * t + hh
                dve.wait_ge(s_mm, s + 1)
                for j in range(2):
                    ins = nc.vector.tensor_reduce(neg_max[:, s, 2 * j:2 * j + 2],
                                                  bank[2 * hh + j][:, 0:2 * CL].rearrange("p (h l) -> p h l", l=CL),
                                                  AX_X, ALU.max, negate=True)
                ins.then_inc(max_ready, 1)

            def inverse(t, hh):
                s = 2 * t + hh
                dve.wait_ge(exp_done, s + 1)
                nc.vector.reciprocal(inv_sum[:, s, :], row_sum[:, s, :]).then_inc(inv_ready, 1)

            def evac_pt(t, g):
                c0, n = GROUPS[g]
                dve.wait_ge(pt_mm, 3 * t + g + 1)
                if g == 1 and t >= 2:
                    dve.wait_ge(pv_mm, t - 1)
                src = bank[5]
                if g == 1:
                    nc.vector.tensor_copy(probsT[:, t % 2, c0:c0 + n, :],
                                          src[:].rearrange("p (c d) -> p c d", d=P)).then_inc(pt_evac, 1)
                else:
                    nc.vector.tensor_copy(probsT[:, t % 2, 8, :], src[:, 0:P])
                    nc.vector.tensor_copy(probsT[0:rows_of(9), t % 2, 9, :],
                                          src[0:rows_of(9), P:2 * P]).then_inc(pt_evac, 1)

            def residual2(t):
                dve.wait_ge(pv_mm, t + 1)
                nc.vector.tensor_tensor(x_tok[:, t, :], x_tok[:, t, :], bank[6 + t % 2][:, 0:D],
                                        ALU.add).then_inc(x2_ready, 1)
                dve.wait_ge(x2_ready, t + 1)
                moments_of(t, t + 1)

            def split_xt3(t):
                cols = slice(t * P, (t + 1) * P)
                dve.wait_ge(xt3_mm, t + 1)
                nc.vector.tensor_copy(x_hi[:, cols], bank[4 + (t == TILES - 1)][:, 0:P]).then_inc(xt3_hi, 1)
                dve.wait_ge(xt3_hi, t + 1)
                nc.vector.tensor_tensor(x_lo[:, cols], bank[4 + (t == TILES - 1)][:, 0:P], f32(x_hi[:, cols]),
                                        ALU.subtract).then_inc(xt3_lo, 1)

            def top2(t):
                dve.wait_ge(logit_mm, t + 1)
                nc.vector.tensor_copy(logits[:, t, :], bank[6 + t % 2][:, D:D + E]).then_inc(logit_read, 1)
                dve.wait_ge(logit_read, t + 1)
                step(nc.vector.max(top_v[:, t, :], logits[:, t, :]))
                settle()
                step(nc.vector.max_index(top_i[:, t, :], top_v[:, t, :], logits[:, t, :]))

            row_max(0, 0)
            row_max(0, 1)
            low_half_x(1)
            inverse(0, 0)
            row_max(1, 0)
            inverse(0, 1)
            row_max(1, 1)
            inverse(1, 0)
            dve.wait_ge(bo_added, 1)
            for t in range(TILES + 2):
                if t < TILES:
                    evac_pt(t, 1)
                if t + 1 < TILES:
                    inverse(t + 1, 1)
                if t + 2 < TILES:
                    row_max(t + 2, 0)
                if 2 <= t < TILES + 2:
                    normalise(2 * BATCH + t - 2, t - 2, t - 1)
                if t < TILES:
                    evac_pt(t, 2)
                if 2 <= t < TILES + 2:
                    split_xt3(t - 2)
                if t + 2 < TILES:
                    row_max(t + 2, 1)
                    inverse(t + 2, 0)
                if 1 <= t <= TILES:
                    residual2(t - 1)
                if 2 <= t < TILES + 2:
                    top2(t - 2)
            settle()
            nc.vector.tensor_tensor(gap[:], top_v[:, :, 1], top_v[:, :, 0], ALU.subtract).then_inc(gap_ready, 1)
            ids = expert_ids[:].unsqueeze(2).broadcast_to([P, E, TILES])
            dve.wait_ge(consts, 6)
            for mask, place in ((mask1, 0), (mask2, 1)):
                step(nc.vector.tensor_tensor(mask[:], ids, top_i[:, :, place].unsqueeze(1).broadcast_to([P, E, TILES]),
                                             ALU.is_equal))
            def gated_up(u, k, least):
                dve.wait_ge(sil_ready, u + 1)
                dve.wait_ge(h2_mm, u + 1)
                if least >= 2:
                    dve.wait_ge(hid_ready, u - 1)
                nc.vector.tensor_tensor(prod[:, k % 2, :], sil[:, k % 2, :], bank[2 + k % 2][:],
                                        ALU.mult).then_inc(prod_ready, 1)

            def low_half(u, k):
                dve.wait_ge(hi_ready, u + 1)
                nc.vector.tensor_tensor(hid_lo[:, k, :], hidden[:, k % 2, :], f32(hid_hi[:, k, :]),
                                        ALU.subtract).then_inc(lo_ready, 1)

            def split_next(n, k, par):
                dve.wait_ge(w_split_hi, 3 * n + (k - 3))
                part = slice((k - 1) * H, k * H)
                nc.vector.tensor_tensor(w_lo[par][:, part], w_raw[par][:, part], f32(w_hi[par][:, part]),
                                        ALU.subtract).then_inc(w_split_lo, 1)

            def route_shares():
                dve.wait_ge(second_ready, 1)
                step(nc.vector.tensor_scalar(norm1[:], second[:], 1.0, None, ALU.add))
                settle()
                step(nc.vector.reciprocal(p1[:], norm1[:]))
                settle()
                step(nc.vector.tensor_tensor(p2[:], second[:], p1[:], ALU.mult))
                step(nc.vector.tensor_tensor(mask1[:], mask1[:], p1[:].unsqueeze(1).broadcast_to([P, E, TILES]), ALU.mult))
                settle()
                step(nc.vector.tensor_tensor(mask2[:], mask2[:], p2[:].unsqueeze(1).broadcast_to([P, E, TILES]), ALU.mult))
                settle()
                nc.vector.tensor_tensor(w_tok[:], mask1[:], mask2[:], ALU.add).then_inc(w_tok_ready, 1)
                dve.wait_ge(w_mm, 1)
                nc.vector.tensor_copy(w_rows[:], bank[4][0:E * TILES, 0:P]).then_inc(w_rows_ready, 1)

            def stages(n, par, first, last):
                for k in range(UPE):
                    u = UPE * n + k
                    least = k if first else UPE + k
                    gated_up(u, k, least)
                    if first and k == 0:
                        route_shares()
                    if least >= 1:
                        low_half(u - 1, (k - 1) % UPE)
                    if k >= 1 and not first and not last:
                        split_next(n, k, 1 - par)

            stages(0, 0, True, False)
            with dve.Fori(0, E // 2 - 1) as i:
                stages(2 * i + 1, 1, False, False)
                stages(2 * i + 2, 0, False, False)
            stages(E - 1, 1, False, False)
            stages(E, 0, False, True)

            def residual3(b):
                tiles = slice(b * TPB, (b + 1) * TPB)
                dve.wait_ge(fin_mm, b + 1)
                nc.vector.tensor_tensor(x_tok[:, tiles, :], x_tok[:, tiles, :],
                                        bank[4 + b][:].rearrange("p (t d) -> p t d", d=D), ALU.add).then_inc(out_ready, 1)

            low_half(UNITS - 1, UPE - 1)
            residual3(0)
            residual3(1)

        @block.tensor
        def _(pe):
            pe.wait_ge(consts, 6)

            def turn(dst, src, n=P):
                return nc.tensor.transpose(dst, src, ident[0:n, 0:n])

            def prep_wait(r):
                if r >= 4:
                    pe.wait_ge(prep_evac, r - 3)
                if r == 4:
                    pe.wait_ge(prep_lo, 1)
                if 14 <= r < 22:
                    pe.wait_ge(prep_lo, r - 12)

            def project_ctx(r, hi, lo):
                c = slice((r - 1) % 4 * P, ((r - 1) % 4 + 1) * P)
                prep_wait(r)
                split_product(nc, bank[r % 4][:, 0:CTX_ROWS], (hi[:, c], lo[:, c]),
                              (ctxT_hi[:], ctxT_lo[:])).then_inc(prep_mm, 1)

            def merge(r, w, kv):
                h = (r - 10) % HEADS
                prep_wait(r)
                rows = slice((h % 2) * DH, (h % 2 + 1) * DH)
                nc.tensor.matmul(bank[r % 4][:, 0:CTX_ROWS], w[rows, h // 2, :], kv[rows, h // 2, :],
                                 start=True, stop=True).then_inc(prep_mm, 1)

            def turn_tiles(n, b):
                pe.wait_ge(xn_ready, n + 1)
                if n >= 2:
                    pe.wait_ge(gate_ready, b + 1)
                dst = bank[4 + b] if n < 2 else z_bank[b]
                for t in range(TPB):
                    ins = turn(dst[:, t * P:(t + 1) * P], xn[:, b * TPB + t, :])
                ins.then_inc(xt_mm, 1)

            def gate_inputs(b):
                cols = slice(b * SEQ, (b + 1) * SEQ)
                pe.wait_ge(wzh_in, 64)
                pe.wait_ge(xt_evac, b + 1)
                nc.tensor.matmul(z_bank[b][:], wz[:], xnT[:, cols], start=True, stop=True).then_inc(z_mm, 1)
                nc.tensor.matmul(h_bank[b][:], wh[:], xnT[:, cols], start=True, stop=True).then_inc(hh_mm, 1)

            def out_gate(b):
                if b == 0:
                    pe.wait_ge(wg_in, 16)
                pe.wait_ge(z_ready, b + 1)
                pe.wait_ge(scan_ready, b + 1)
                nc.tensor.matmul(z_bank[b][:], wg[:], hT[:, b * SEQ:(b + 1) * SEQ],
                                 start=True, stop=True).then_inc(gate_mm, 1)

            def turn_y(b):
                pe.wait_ge(y_ready, b + 1)
                pe.wait_ge(scan_ready, b + 1)
                for t in range(TPB):
                    ins = turn(h_bank[b][:, t * P:(t + 1) * P], yT[:, b * SEQ + t * P:b * SEQ + (t + 1) * P])
                ins.then_inc(ytok_mm, 1)

            def turn_u(b):
                flat = UT[:, b, :, :].rearrange("p h l -> p (h l)")
                for g, (c0, n) in enumerate(GROUPS):
                    q = 3 * b + g
                    if q == 0:
                        pe.wait_ge(prep_evac, 26)
                        pe.wait_ge(x1_ready, 2)
                    if q >= 2:
                        pe.wait_ge(u_evac, q - 1)
                    for c in range(c0, c0 + n):
                        m = rows_of(c)
                        ins = turn(h_bank[q % 2][0:m, (c - c0) * P:(c - c0) * P + P], flat[:, c * P:c * P + m])
                    ins.then_inc(u_mm, 1)

            pe.wait_ge(ctx_in_s, 16)
            for c in range(CTX_CUT):
                ins = turn(bank[0][0:CTX, c * CTX_TILE:(c + 1) * CTX_TILE], ctx_rows[:, c, :], CTX_TILE)
            ins.then_inc(prep_mm, 1)
            turn_tiles(0, 0)
            pe.wait_ge(wkv_lo, 1)
            pe.wait_ge(prep_lo, 1)
            project_ctx(1, wk_hi, wk_lo)
            turn_tiles(1, 1)
            gate_inputs(0)
            project_ctx(2, wk_hi, wk_lo)
            gate_inputs(1)
            project_ctx(3, wk_hi, wk_lo)
            project_ctx(4, wk_hi, wk_lo)
            out_gate(0)
            pe.wait_ge(wkv_lo, 2)
            project_ctx(5, wv_hi, wv_lo)
            project_ctx(6, wv_hi, wv_lo)
            out_gate(1)
            project_ctx(7, wv_hi, wv_lo)
            project_ctx(8, wv_hi, wv_lo)
            turn_y(0)
            pe.wait_ge(wq_in, 16)
            prep_wait(9)
            for c in range(4):
                ins = turn(bank[1][:, c * P:(c + 1) * P], wq[:, c * P:(c + 1) * P])
            ins.then_inc(prep_mm, 1)
            turn_y(1)
            pe.wait_ge(prep_evac, 10)
            for r in range(10, 18):
                merge(r, wqT, kT)
            turn_tiles(2, 0)
            pe.wait_ge(wo_in, 16)
            for r in range(18, 26):
                merge(r, wo, vT)

            def scores(t, hh):
                s = 2 * t + hh
                if t >= 1:
                    pe.wait_ge(exp_done, s - 1)
                elif hh == 0:
                    pe.wait_ge(prep_evac, 26)
                    pe.wait_ge(prep_lo, 9)
                if t % TPB == 0 and hh == 0:
                    pe.wait_ge(x_lo_ready, 1 + t // TPB)
                cols = slice(t * P, (t + 1) * P)
                for j in range(2):
                    h0 = hh * HPU + 2 * j
                    rhs = [a[:, t // TPB, h0:h0 + 2, :].rearrange("p h l -> p (h l)") for a in (A_hi, A_lo)]
                    ins = split_product(nc, bank[2 * hh + j][:, 0:2 * CL], (x_hi[:, cols], x_lo[:, cols]), rhs)
                ins.then_inc(s_mm, 1)

            def turn_probs(t, g):
                if g == 0:
                    pe.wait_ge(pn_ready, 2 * t + 2)
                    if t == 0:
                        pe.wait_ge(x_lo_ready, 2)
                    if t >= 1:
                        pe.wait_ge(pt0_evac, t)
                    if t >= 3:
                        pe.wait_ge(xt3_lo, t - 2)
                if g == 1:
                    if t == 0:
                        pe.wait_ge(u_evac, 6)
                    else:
                        pe.wait_ge(pt_evac, 2 * t)
                if g == 2:
                    pe.wait_ge(pt_evac, 2 * t + 1)
                c0, n = GROUPS[g]
                flat = probs[:, t % 3, :, :].rearrange("p h l -> p (h l)")
                for c in range(c0, c0 + n):
                    m = rows_of(c)
                    ins = turn(bank[4 if g == 0 else 5][0:m, (c - c0) * P:(c - c0) * P + P],
                               flat[:, c * P:c * P + m])
                ins.then_inc(pt_mm, 1)

            def turn_tile3(t):
                pe.wait_ge(xn_ready, 4 + t + 1)
                if t < TILES - 1:
                    pe.wait_ge(pt0_evac, min(t + 3, TILES))
                    turn(bank[4][:, 0:P], xn[:, t, :]).then_inc(xt3_mm, 1)
                else:
                    pe.wait_ge(pt_evac, 2 * TILES)
                    turn(bank[5][:, 0:P], xn[:, t, :]).then_inc(xt3_mm, 1)

            def attend(t, chunks):
                for c in chunks:
                    if c == 0:
                        if t == 0:
                            pe.wait_ge(u_evac, 6)
                        if t >= 2:
                            pe.wait_ge(x2_ready, t - 1)
                            pe.wait_ge(logit_read, t - 1)
                        pe.wait_ge(pt0_evac, t + 1)
                    if c in (4, 8):
                        pe.wait_ge(pt_evac, 2 * t + c // 4)
                    m = rows_of(c)
                    ins = nc.tensor.matmul(bank[6 + t % 2][:, 0:D], probsT[0:m, t % 2, c, :],
                                           U[0:m, t // TPB, c, :], start=(c == 0), stop=(c == NCH - 1))
                if chunks[-1] == NCH - 1:
                    ins.then_inc(pv_mm, 1)

            def route(t):
                if t == 0:
                    pe.wait_ge(gw_split, 2)
                pe.wait_ge(xt3_lo, t + 1)
                pe.wait_ge(x2_ready, t + 1)
                cols = slice(t * P, (t + 1) * P)
                split_product(nc, bank[6 + t % 2][:, D:D + E], (x_hi[:, cols], x_lo[:, cols]),
                              (gw_hi[:], gw_lo[:])).then_inc(logit_mm, 1)

            def up(u, k, par, least):
                n, c = k // HC, k % HC
                cols = slice(n * SEQ, (n + 1) * SEQ)
                if least >= 2:
                    pe.wait_ge(sil_ready, u - 1)
                    pe.wait_ge(prod_ready, u - 1)
                for w0, dst, done in ((0, bank[k % 2], h1_mm), (H, bank[2 + k % 2], h2_mm)):
                    part = slice(w0 + c * P, w0 + (c + 1) * P)
                    split_product(nc, dst[:], (w_hi[par][:, part], w_lo[par][:, part]),
                                  (x_hi[:, cols], x_lo[:, cols])).then_inc(done, 1)

            def down(u, k, par):
                n, c = k // HC, k % HC
                part = slice(2 * H + c * P, 2 * H + (c + 1) * P)
                pe.wait_ge(lo_ready, u + 1)
                split_product(nc, bank[6 + n][:], (w_hi[par][:, part], w_lo[par][:, part]),
                              (hid_hi[:, k, :], hid_lo[:, k, :]), start=False, stop=False,
                              skip_group_check=True).then_inc(o_mm, 1)

            scores(0, 0)
            scores(0, 1)
            turn_u(0)
            turn_tiles(3, 1)
            scores(1, 0)
            turn_u(1)
            scores(1, 1)
            for t in range(TILES + 2):
                if t < TILES:
                    turn_probs(t, 0)
                    turn_probs(t, 1)
                if t + 2 < TILES:
                    scores(t + 2, 0)
                if 1 <= t <= TILES:
                    attend(t - 1, range(0, 5))
                if t < TILES:
                    turn_probs(t, 2)
                if t >= 2:
                    turn_tile3(t - 2)
                if t + 2 < TILES:
                    scores(t + 2, 1)
                if 1 <= t <= TILES:
                    attend(t - 1, range(5, NCH))
                if t >= 2:
                    route(t - 2)
                if t == TILES:
                    pe.wait_ge(first_lo, 2)
                    pe.wait_ge(exp_done, 2 * TILES)
                    up(0, 0, 0, 0)
            up(1, 1, 0, 1)
            pe.wait_ge(w_tok_ready, 1)
            pe.wait_ge(xt3_lo, TILES)
            turn(bank[4][0:E * TILES, 0:P], w_tok[:].rearrange("p e t -> p (e t)")).then_inc(w_mm, 1)
            pe.wait_ge(logit_read, TILES)
            for n in range(BATCH):
                nc.tensor.matmul(bank[6 + n][:], zeros[:, 0:P], zeros[:], start=True, stop=False,
                                 skip_group_check=True)
            up(2, 2, 0, 2)
            up(3, 3, 0, 3)
            down(0, 0, 0)

            def stages(n, par, thirds):
                for k in range(UPE):
                    u = UPE * n + k
                    if k == 0 and thirds is not None:
                        pe.wait_ge(w_split_lo, thirds + 2)
                    up(u, k, par, UPE)
                    if k == 3 and thirds is not None:
                        pe.wait_ge(w_split_lo, thirds + 3)
                    down(u - 3, (k - 3) % UPE, par if k == 3 else 1 - par)

            stages(1, 1, None)
            with pe.Fori(0, E // 2 - 1) as i:
                stages(2 * i + 2, 0, 6 * i)
                stages(2 * i + 3, 1, 6 * i + 3)
            stages(E, 0, 3 * (E - 2))

            def turn_moe(b):
                pe.wait_ge(moe_evac, b + 1)
                for t in range(TPB):
                    ins = turn(bank[4 + b][:, t * P:(t + 1) * P], moeT[:, b * SEQ + t * P:b * SEQ + (t + 1) * P])
                ins.then_inc(fin_mm, 1)

            down(UNITS - 3, 1, 0)
            down(UNITS - 2, 2, 0)
            pe.wait_ge(w_rows_ready, 1)
            turn_moe(0)
            down(UNITS - 1, 3, 0)
            turn_moe(1)


_INS = ["x", "ctx_768", "L0_attn_W_zf", "L0_attn_b_zf", "L0_attn_W_hf", "L0_attn_b_hf", "L0_attn_W_zs",
        "L0_attn_b_zs", "L0_attn_W_hs", "L0_attn_b_hs", "L0_attn_W_g", "L0_attn_b_g", "L0_xattn_Wq",
        "L0_xattn_Wk", "L0_xattn_Wv", "L0_xattn_Wo", "L0_xattn_bo", "L0_ffn_gate_w", "L0_ffn_ew1",
        "L0_ffn_ew2", "L0_ffn_ew3", "L0_ffn_sw1", "L0_ffn_sw2", "L0_ffn_sw3"]


def kernel(**inputs):
    import numpy as _np
    import concourse.bacc as _bacc
    from concourse import mybir as _mybir
    from concourse.bass_utils import run_bass_kernel_spmd as _run

    nc = _bacc.Bacc("TRN2", target_bir_lowering=False, num_devices=1)
    arrays, args = {}, []
    for name in _INS:
        a = _np.ascontiguousarray(inputs[name])
        arrays[f"in_{name}"] = a
        args.append(nc.dram_tensor(f"in_{name}", a.shape, _mybir.dt.from_np(a.dtype), kind="ExternalInput").ap())
    args.append(nc.dram_tensor("router_scratch", (8, 1024), _mybir.dt.float32).ap())
    args.append(nc.dram_tensor("out_0", (2, 512, 128), _mybir.dt.float32, kind="ExternalOutput").ap())
    decoder_block(nc, *args)
    return _run(nc, [arrays], core_ids=[0]).results[0]["out_0"]
```

```python
import math
from contextlib import ExitStack

import concourse.bass as bass
from concourse import mybir

F32 = mybir.dt.float32
F32R = mybir.dt.float32r
BF16 = mybir.dt.bfloat16
U32 = mybir.dt.uint32
ALU = mybir.AluOpType
ACT = mybir.ActivationFunctionType
AX_X = mybir.AxisListType.X

P = 128
D = 128
BATCH, SEQ = 2, 512
TOK = BATCH * SEQ
TILES = TOK // P
TPB = SEQ // P
CH = 64
CTX, CL = 96, 154
CTX_ROWS = BATCH * CL
HEADS, DH = 8, 64
INNER = HEADS * DH
HPU = 4
REST = CL - P
NCH = HEADS + HEADS // HPU
E, H = 8, 256
HC = H // P
UPE = BATCH * HC
UNITS = (E + 1) * UPE
PIECES = 2
EPS = 1e-5
CTX_CUT = 4
CTX_TILE = CTX_ROWS // CTX_CUT
GROUPS = [(0, 4), (4, 4), (8, 2)]
WAKE = 7
PREP = 22


def rows_of(c):
    return P if c < HEADS else HPU * REST


def pairs_of(c):
    return slice(c * P, (c + 1) * P) if c < HEADS else slice(HEADS * P + (c - HEADS) * HPU * REST,
                                                             HEADS * P + (c - HEADS + 1) * HPU * REST)


def piece_of(j):
    return slice(0, SEQ) if j is None else slice(j * SEQ // PIECES, (j + 1) * SEQ // PIECES)


def f32(ap):
    return ap.bitcast(F32)


def split_product(nc, dst, lhs, rhs, start=True, stop=True, **kw):
    nc.tensor.matmul(dst, lhs[0], rhs[0], start=start, stop=False, **kw)
    nc.tensor.matmul(dst, lhs[0], rhs[1], start=False, stop=False, **kw)
    return nc.tensor.matmul(dst, lhs[1], rhs[0], start=False, stop=stop, **kw)


def decoder_block(nc, x, ctx_in, w_zf, b_zf, w_hf, b_hf, w_zs, b_zs, w_hs, b_hs, w_g, b_g,
                  w_q, w_k, w_v, w_o, b_o, w_gate, ew1, ew2, ew3, sw1, sw2, sw3, scratch, out):
    with ExitStack() as ctx:
        def sb(name, shape, dt=F32):
            return ctx.enter_context(nc.sbuf_tensor(name, shape, dt))

        def sem(name):
            return ctx.enter_context(nc.semaphore(name))

        bank = [ctx.enter_context(nc.psum_tensor(f"bank{i}", [P, 512], F32)) for i in range(8)]

        ident = sb("ident", [P, P])
        minus_half = sb("minus_half", [P, TILES])
        euler = sb("euler", [P, TILES])
        zeros = sb("zeros", [P, 512], BF16)
        expert_ids = sb("expert_ids", [P, E])
        x_tok = sb("x_tok", [P, TILES, D])
        xn = sb("xn", [P, TILES, D])
        stats = sb("stats", [P, TILES, 6])
        moments = sb("moments", [P, TILES, 2])
        var_eps = sb("var_eps", [P, TILES])
        rstd = sb("rstd", [P, TILES])
        xnT = sb("xnT", [P, TOK])
        x_hi, x_lo = sb("x_hi", [P, TOK], F32R), sb("x_lo", [P, TOK], F32R)
        wz, wh, wg = sb("wz", [P, P]), sb("wh", [P, P]), sb("wg", [P, P])
        bz, bh, bg = sb("bz", [P, 1]), sb("bh", [P, 1]), sb("bg", [P, 1])
        zT, decayT, driveT = sb("zT", [P, TOK]), sb("decayT", [P, TOK]), sb("driveT", [P, TOK])
        hT, yT = sb("hT", [P, TOK]), sb("yT", [P, TOK])
        gateT = zT
        ctx_rows = sb("ctx_rows", [CTX_TILE, CTX_CUT, CTX])
        ctxT = sb("ctxT", [CTX, CTX_ROWS])
        wq, wk, wv = sb("wq", [P, INNER]), sb("wk", [CTX, INNER]), sb("wv", [CTX, INNER])
        wo = sb("wo", [P, 4, D])
        wqT = sb("wqT", [P, 4, D])
        wkT, wvT = sb("wkT", [P, 4, CTX]), sb("wvT", [P, 4, CTX])
        M, N = sb("M", [CTX, HEADS, D]), sb("N", [CTX, HEADS, D])
        UT_rest = sb("UT_rest", [P, BATCH, HEADS, REST])
        A_hi, A_lo = sb("A_hi", [P, BATCH, HEADS, CL], F32R), sb("A_lo", [P, BATCH, HEADS, CL], F32R)
        U = sb("U", [P, BATCH, NCH, D])
        bo_rows = sb("bo_rows", [P, D])
        exps_tok = sb("exps_tok", [P, 2, HEADS, CL])
        probs_n = sb("probs_n", [P, 2, HEADS * CL])
        neg_max = sb("neg_max", [P, 2 * TILES, HPU])
        row_sum = sb("row_sum", [P, 2 * TILES, HPU])
        inv_sum = sb("inv_sum", [P, 2 * TILES, HPU])
        probsT = sb("probsT", [P, 2, NCH, P])
        gate_w = sb("gate_w", [P, E])
        gw = sb("gw", [P, 2 * E], F32R)
        logits = sb("logits", [P, TILES, E])
        top_v = sb("top_v", [P, TILES, 8])
        top_i = sb("top_i", [P, TILES, 8], U32)
        gap, second = sb("gap", [P, BATCH, TPB]), sb("second", [P, BATCH, TPB])
        norm1, p1, p2 = (sb(n, [P, BATCH, TPB]) for n in ("norm1", "p1", "p2"))
        mask1, mask2 = sb("mask1", [P, BATCH, E, TPB]), sb("mask2", [P, BATCH, E, TPB])
        w_tok = sb("w_tok", [P, BATCH, E, TPB])
        w_rows = sb("w_rows", [E * TPB, BATCH, P])
        share = [sb(f"share{p}", [P, TOK]) for p in range(2)]
        w_raw = [sb(f"w_raw{p}", [P, 3 * H]) for p in range(2)]
        w_hi = [sb(f"w_hi{p}", [P, 3 * H], F32R) for p in range(2)]
        w_lo = [sb(f"w_lo{p}", [P, 3 * H], F32R) for p in range(2)]
        sil, prod = sb("sil", [P, 2, 512]), sb("prod", [P, 2, 512])
        hidden = sb("hidden", [P, 2, 512])
        hid_hi, hid_lo = sb("hid_hi", [P, UPE, 512], F32R), sb("hid_lo", [P, UPE, 512], F32R)
        moeT = sb("moeT", [P, TOK])

        z_bank, h_bank = (bank[6], bank[4]), (bank[7], bank[5])
        prep_bank = [bank[i] for i in (0, 1, 2, 3, 0, 1, 2, 3, 0, 1, 2, 3, 4, 7, 2, 3)]
        xt2_bank = (bank[6], bank[7])
        u_bank = (bank[6], bank[7], bank[6], bank[6], bank[6], bank[7])

        x_in = [sem(f"x_in{b}") for b in range(BATCH)]
        wzh_in, wg_in, bias_in, ctx_in_s, bo_in, gw_in = (
            sem(n) for n in ("wzh_in", "wg_in", "bias_in", "ctx_in", "bo_in", "gw_in"))
        wk_in, wv_in, wq_in, wo_in = (sem(n) for n in ("wk_in", "wv_in", "wq_in", "wo_in"))
        consts = sem("consts")
        dve_step = sem("dve_step")
        var_ready, rstd_ready, xn_ready = sem("var_ready"), sem("rstd_ready"), sem("xn_ready")
        xt_mm, xt_evac = sem("xt_mm"), sem("xt_evac")
        z_mm, hh_mm, z_ready, scan_ready = (sem(n) for n in ("z_mm", "hh_mm", "z_ready", "scan_ready"))
        gate_mm, gate_ready, y_ready, ytok_mm, x1_ready = (
            sem(n) for n in ("gate_mm", "gate_ready", "y_ready", "ytok_mm", "x1_ready"))
        prep_mm, prep_evac, prep_lo = sem("prep_mm"), sem("prep_evac"), sem("prep_lo")
        gw_split, first_hi, first_lo = (sem(n) for n in ("gw_split", "first_hi", "first_lo"))
        x_lo_ready, bo_added, w_split_hi, w_split_lo = (
            sem(n) for n in ("x_lo_ready", "bo_added", "w_split_hi", "w_split_lo"))
        ones_ready = sem("ones_ready")
        hi_ready, lo_ready = sem("hi_ready"), sem("lo_ready")
        s_mm, max_ready, exp_done, inv_ready, pn_ready = (
            sem(n) for n in ("s_mm", "max_ready", "exp_done", "inv_ready", "pn_ready"))
        pt_mm, pt0_evac, pt_evac, pv_mm, x2_ready = (
            sem(n) for n in ("pt_mm", "pt0_evac", "pt_evac", "pv_mm", "x2_ready"))
        xt3_mm, xt3_hi, xt3_lo = (sem(n) for n in ("xt3_mm", "xt3_hi", "xt3_lo"))
        logit_mm, logit_read, gap_ready, second_ready = (
            sem(n) for n in ("logit_mm", "logit_read", "gap_ready", "second_ready"))
        w_tok_ready, w_mm, w_rows_ready, w_stored = (
            sem(n) for n in ("w_tok_ready", "w_mm", "w_rows_ready", "w_stored"))
        share_in = [[sem(f"share_in{p}_{b}") for b in range(BATCH)] for p in range(2)]
        ew_in = [sem(f"ew_in{p}") for p in range(2)]
        h1_mm, h2_mm, o_mm, sil_ready, prod_ready, hid_ready = (
            sem(n) for n in ("h1_mm", "h2_mm", "o_mm", "sil_ready", "prod_ready", "hid_ready"))
        moe_evac, fin_mm, out_ready, stored = (
            sem(n) for n in ("moe_evac", "fin_mm", "out_ready", "stored"))

        x_view = x.rearrange("b (t p) d -> b p t d", p=P)
        out_view = out.rearrange("b (t p) d -> b p t d", p=P)
        col = lambda v: v.rearrange("(n a) -> n a", a=1)
        row = lambda v: v.rearrange("(a n) -> a n", a=1)

        block = ctx.enter_context(nc.Block())

        @block.sync
        def _(sp):
            def load_expert(p, a1, a2, a3):
                sp.dma_start(w_raw[p][:, 0:H], a1).then_inc(ew_in[p], 16)
                sp.dma_start(w_raw[p][:, H:2 * H], a2).then_inc(ew_in[p], 16)
                sp.dma_start(w_raw[p][:, 2 * H:3 * H].rearrange("p (c n) -> p c n", c=HC),
                             a3.rearrange("(c p) n -> p c n", p=P)).then_inc(ew_in[p], 16)

            def load_share_half(p, e, b):
                sp.dma_start(share[p][:, b * SEQ:(b + 1) * SEQ],
                             scratch[b, bass.ds(e, 1), :].broadcast_to([P, SEQ])).then_inc(share_in[p][b], 16)

            def load_share(p, e):
                for b in range(BATCH):
                    load_share_half(p, e, b)

            for b in range(BATCH):
                sp.dma_start(x_tok[:, b * TPB:(b + 1) * TPB, :], x_view[b]).then_inc(x_in[b], 16)
            sp.dma_start(wz[:, 0:CH], w_zf).then_inc(wzh_in, 16)
            sp.dma_start(wz[:, CH:P], w_zs).then_inc(wzh_in, 16)
            sp.dma_start(wh[:, 0:CH], w_hf).then_inc(wzh_in, 16)
            sp.dma_start(wh[:, CH:P], w_hs).then_inc(wzh_in, 16)
            sp.dma_start(bz[0:CH, :], col(b_zf)).then_inc(bias_in, 16)
            sp.dma_start(bz[CH:P, :], col(b_zs)).then_inc(bias_in, 16)
            sp.dma_start(bh[0:CH, :], col(b_hf)).then_inc(bias_in, 16)
            sp.dma_start(bh[CH:P, :], col(b_hs)).then_inc(bias_in, 16)
            sp.dma_start(bg[:], col(b_g)).then_inc(bias_in, 16)
            sp.dma_start(wg[:], w_g).then_inc(wg_in, 16)
            sp.dma_start(wo[:], w_o.rearrange("(c p) n -> p c n", p=P)).then_inc(wo_in, 16)
            sp.dma_start(gate_w[:], w_gate).then_inc(gw_in, 16)
            load_expert(0, sw1, sw2, sw3)
            load_expert(1, ew1[0], ew2[0], ew3[0])
            sp.dma_start(bo_rows[:], row(b_o).broadcast_to([P, D])).then_inc(bo_in, 16)
            sp.wait_ge(first_lo, 1)
            load_expert(0, ew1[1], ew2[1], ew3[1])
            for b in range(BATCH):
                sp.wait_ge(w_rows_ready, b + 1)
                sp.dma_start(scratch[b].rearrange("e (t p) -> (e t) p", p=P), w_rows[:, b, :]).then_inc(w_stored, 16)
                sp.wait_ge(w_stored, 16 * (b + 1))
                load_share_half(1, 0, b)
            sp.wait_ge(w_split_lo, 3)
            load_expert(1, ew1[2], ew2[2], ew3[2])
            sp.wait_ge(hid_ready, UPE)
            load_share(0, 1)

            with sp.Fori(0, 2) as i:
                for j in range(2):
                    n = 2 * i + (4 + j)
                    sp.wait_ge(w_split_lo, 6 * i + (6 + 3 * j))
                    load_expert(j, ew1[n - 1], ew2[n - 1], ew3[n - 1])
                    sp.wait_ge(hid_ready, 8 * i + (8 + 4 * j))
                    load_share(1 - j, n - 2)
            sp.wait_ge(w_split_lo, 3 * (E - 2))
            load_expert(0, ew1[E - 1], ew2[E - 1], ew3[E - 1])
            for n in (E - 1, E):
                sp.wait_ge(hid_ready, UPE * (n - 1))
                load_share(n % 2, n - 1)
            sp.wait_ge(out_ready, 1)
            sp.dma_start(out_view[0], x_tok[:, 0:TPB, :]).then_inc(stored, 16)
            for piece in range(PIECES):
                t0, t1 = piece_of(piece).start // P, piece_of(piece).stop // P
                sp.wait_ge(out_ready, 2 + piece)
                sp.dma_start(out_view[1][:, t0:t1, :], x_tok[:, TPB + t0:TPB + t1, :]).then_inc(stored, 16)
            sp.wait_ge(stored, 16 * (1 + PIECES))

        @block.gpsimd
        def _(pool):
            nc.gpsimd.memset(ident[:], 0.0).then_inc(consts, 1)
            nc.gpsimd.memset(minus_half[:], -0.5).then_inc(consts, 1)
            nc.gpsimd.memset(euler[:], math.e).then_inc(consts, 1)
            nc.gpsimd.iota(expert_ids[:], pattern=[[1, E]], base=0, channel_multiplier=0,
                           allow_small_or_imprecise_dtypes=True).then_inc(consts, 1)
            nc.gpsimd.memset(zeros[:], 0.0).then_inc(consts, 1)
            pool.wait_ge(consts, 5)
            nc.gpsimd.affine_select(out=ident[:], in_=ident[:], compare_op=ALU.not_equal, fill=1.0,
                                    base=0, pattern=[[-1, P]], channel_multiplier=1).then_inc(consts, 1)
            pool.wait_ge(consts, 6)

            def rsqrt(n, t0, t1):
                pool.wait_ge(var_ready, n + 1)
                nc.gpsimd.tensor_tensor(rstd[:, t0:t1], var_eps[:, t0:t1], minus_half[:, t0:t1],
                                        ALU.pow).then_inc(rstd_ready, 1)

            rsqrt(0, 0, TPB)
            rsqrt(1, TPB, TILES)
            pool.wait_ge(gw_in, 16)
            nc.gpsimd.tensor_copy(gw[:, 0:E], gate_w[:]).then_inc(gw_split, 1)
            pool.wait_ge(gw_split, 1)
            nc.gpsimd.tensor_tensor(gw[:, E:2 * E], gate_w[:], f32(gw[:, 0:E]), ALU.subtract).then_inc(gw_split, 1)
            nc.gpsimd.memset(share[0][:], 1.0).then_inc(ones_ready, 1)
            pool.wait_ge(ew_in[0], 48)
            nc.gpsimd.tensor_copy(w_hi[0][:], w_raw[0][:]).then_inc(first_hi, 1)
            pool.wait_ge(first_hi, 1)
            nc.gpsimd.tensor_tensor(w_lo[0][:], w_raw[0][:], f32(w_hi[0][:]), ALU.subtract).then_inc(first_lo, 1)
            rsqrt(2, 0, TPB)

            def add_bias(b):
                tiles = slice(b * TPB, (b + 1) * TPB)
                pool.wait_ge(bo_in, 16)
                pool.wait_ge(xn_ready, 3 + b)
                nc.gpsimd.tensor_tensor(x_tok[:, tiles, :], x_tok[:, tiles, :],
                                        bo_rows[:].unsqueeze(1).broadcast_to([P, TPB, D]),
                                        ALU.add).then_inc(bo_added, 1)

            add_bias(0)

            def second_power(b):
                pool.wait_ge(gap_ready, b + 1)
                nc.gpsimd.tensor_tensor(second[:, b, :], euler[:, 0:TPB], gap[:, b, :],
                                        ALU.pow).then_inc(second_ready, 1)

            def normalise(t, hh):
                s = 2 * t + hh
                pool.wait_ge(inv_ready, s + 1)
                if t >= 2:
                    pool.wait_ge(pt_mm, 3 * (t - 1))
                inv = inv_sum[:, s, :].unsqueeze(2)
                for positions, cols in ((slice(0, P), slice(hh * HPU * P, (hh + 1) * HPU * P)),
                                        (slice(P, CL), pairs_of(HEADS + hh))):
                    n = positions.stop - positions.start
                    ins = nc.gpsimd.tensor_tensor(
                        probs_n[:, t % 2, cols].rearrange("p (h l) -> p h l", h=HPU),
                        exps_tok[:, t % 2, hh * HPU:(hh + 1) * HPU, positions],
                        inv.broadcast_to([P, HPU, n]), ALU.mult)
                ins.then_inc(pn_ready, 1)

            def weigh(u, k, par, least, piece=None):
                cols, shift = piece_of(piece), piece or 0
                first = k // HC * SEQ + cols.start
                pool.wait_ge(prod_ready, u + 1 + shift)
                if least >= 2 and not piece:
                    pool.wait_ge(lo_ready, u - 1)
                nc.gpsimd.tensor_tensor(hidden[:, k % 2, cols], prod[:, k % 2, cols],
                                        share[par][:, first:first + cols.stop - cols.start],
                                        ALU.mult).then_inc(hid_ready, 1)

            normalise(0, 0)
            normalise(0, 1)
            rsqrt(3, TPB, TILES)
            normalise(1, 0)
            for t in range(TILES + 2):
                if t >= 2:
                    rsqrt(2 * BATCH + t - 2, t - 2, t - 1)
                if t + 1 < TILES:
                    normalise(t + 1, 1)
                if t + 2 < TILES:
                    normalise(t + 2, 0)
                if t == 0:
                    add_bias(1)
                if t == TILES - 2:
                    second_power(0)
                if t == TILES - 1:
                    for k in range(1, UPE):
                        pool.wait_ge(w_split_hi, k)
                        part = slice((k - 1) * H, k * H)
                        nc.gpsimd.tensor_tensor(w_lo[1][:, part], w_raw[1][:, part], f32(w_hi[1][:, part]),
                                                ALU.subtract).then_inc(w_split_lo, 1)
                if t == TILES:
                    pool.wait_ge(ones_ready, 1)
                if t >= TILES:
                    weigh(t - TILES, t - TILES, 0, t - TILES)

            def weigh_expert(n, par, uses, last=False):
                for k in range(UPE):
                    if k % HC == 0:
                        pool.wait_ge(share_in[par][k // HC], uses)
                    if last and k == UPE - 1:
                        for piece in range(PIECES):
                            weigh(UPE * n + k, k, par, UPE, piece)
                    else:
                        weigh(UPE * n + k, k, par, UPE)

            second_power(1)
            for k in (2, 3):
                weigh(k, k, 0, k)
            with pool.Fori(0, E // 2 - 1) as i:
                weigh_expert(2 * i + 1, 1, 16 * i + 16)
                weigh_expert(2 * i + 2, 0, 16 * i + 16)
            weigh_expert(E - 1, 1, 16 * (E // 2))
            weigh_expert(E, 0, 16 * (E // 2), last=True)

        @block.scalar
        def _(act):
            act.dma_start(ctx_rows[:], ctx_in.rearrange("b l c -> (b l) c").rearrange("(c p) n -> p c n", p=CTX_TILE)
                          ).then_inc(ctx_in_s, 16)
            act.dma_start(wk[:], w_k).then_inc(wk_in, 16)
            act.preload_act_table(ACT.Sigmoid)
            act.dma_start(wq[:], w_q).then_inc(wq_in, 16)
            act.dma_start(wv[:], w_v).then_inc(wv_in, 16)

            def copy(dst, src, scale=1.0):
                return nc.scalar.activation(dst, src, ACT.Copy, scale=scale)

            def prep(r, dst, src, scale=1.0):
                act.wait_ge(prep_mm, r + 1)
                copy(dst, src, scale).then_inc(prep_evac, 1)

            def prep_turned(r, wT, width, scale=1.0):
                prep(r, wT[:].rearrange("p c d -> p (c d)"), prep_bank[r][:, 0:width], scale)

            def prep_mn(r, mn):
                prep(r, mn[:, r % 2 * HPU:(r % 2 + 1) * HPU, :],
                     prep_bank[r][0:CTX, :].rearrange("p (h d) -> p h d", d=D))

            def prep_a(r):
                prep(r, A_hi[:, :, r - 8, :], prep_bank[r][:, 0:CTX_ROWS].rearrange("p (b l) -> p b l", b=BATCH))

            def prep_u(r):
                src = u_bank[r - 16]
                if r == 18:
                    prep(r, UT_rest[:].rearrange("p b h l -> p h b l"),
                         src[:, 0:BATCH * HEADS * REST].rearrange("p (h b l) -> p h b l", h=HEADS, b=BATCH))
                elif r == 19:
                    m = HPU * REST
                    prep(r, U[0:m, :, HEADS:NCH, :], src[0:m, :].rearrange("p (b c d) -> p b c d", b=BATCH, d=D))
                else:
                    b, g = (r - 16) // 4, r % 2
                    prep(r, U[:, b, g * HPU:(g + 1) * HPU, :], src[:].rearrange("p (c d) -> p c d", d=D))

            def forget_gate(b):
                act.wait_ge(z_mm, b + 1)
                nc.scalar.activation(zT[:, b * SEQ:(b + 1) * SEQ], z_bank[b][:], ACT.Sigmoid,
                                     bias=bz[:, 0:1]).then_inc(z_ready, 1)

            def out_gate(b):
                act.wait_ge(gate_mm, b + 1)
                nc.scalar.activation(gateT[:, b * SEQ:(b + 1) * SEQ], z_bank[b][:], ACT.Sigmoid,
                                     bias=bg[:, 0:1]).then_inc(gate_ready, 1)

            def evac_xt(n, b, dst):
                act.wait_ge(xt_mm, n + 1)
                src = bank[4 + b] if n < 2 else xt2_bank[b]
                copy(dst[:, b * SEQ:(b + 1) * SEQ], src[:]).then_inc(xt_evac, 1)

            prep(0, ctxT[:], bank[0][0:CTX, 0:CTX_ROWS])
            prep_turned(1, wkT, 4 * CTX)
            prep_turned(2, wqT, 4 * D, scale=DH ** -0.5)
            evac_xt(0, 0, xnT)
            prep_turned(3, wvT, 4 * CTX)
            act.wait_ge(bias_in, 80)
            forget_gate(0)
            evac_xt(1, 1, xnT)
            prep_mn(4, M)
            forget_gate(1)
            out_gate(0)
            prep_mn(5, M)
            prep_mn(6, N)
            out_gate(1)
            prep_mn(7, N)
            for r in range(8, 13):
                prep_a(r)
            evac_xt(2, 0, x_hi)
            for r in range(13, 16):
                prep_a(r)
            act.preload_act_table(ACT.Exp)

            def exps(t, hh):
                s = 2 * t + hh
                act.wait_ge(max_ready, s + 1)
                if t >= 2:
                    act.wait_ge(pn_ready, s - 3)
                for q in range(HPU):
                    ins = nc.scalar.activation(exps_tok[:, t % 2, hh * HPU + q, :],
                                               bank[2 * hh + q // 2][:, (q % 2) * CL:(q % 2 + 1) * CL], ACT.Exp,
                                               bias=neg_max[:, s, q:q + 1], accum_out=row_sum[:, s, q:q + 1])
                ins.then_inc(exp_done, 1)

            def evac_pt(t):
                act.wait_ge(pt_mm, 3 * t + 1)
                if t >= 2:
                    act.wait_ge(pv_mm, t - 1)
                copy(probsT[:, t % 2, 0:4, :], bank[4][:].rearrange("p (c d) -> p c d", d=P)).then_inc(pt0_evac, 1)

            exps(0, 0)
            prep_u(16)
            exps(0, 1)
            prep_u(17)
            prep_u(18)
            exps(1, 0)
            for t in range(TILES):
                evac_pt(t)
                if t == 0:
                    exps(1, 1)
                    prep_u(19)
                if t == 1:
                    evac_xt(3, 1, x_hi)
                if t + 2 < TILES:
                    exps(t + 2, 0)
                if t == 0:
                    prep_u(20)
                if t + 2 < TILES:
                    exps(t + 2, 1)
                if t == 1:
                    prep_u(21)
            act.preload_act_table(ACT.Silu)

            def silu(u, k, least):
                act.wait_ge(h1_mm, u + 1)
                if least >= 2:
                    act.wait_ge(prod_ready, u - 1)
                nc.scalar.activation(sil[:, k % 2, :], bank[k % 2][:], ACT.Silu).then_inc(sil_ready, 1)

            def high_half(u, k, least, piece=None):
                cols = piece_of(piece)
                act.wait_ge(hid_ready, u + 1 + (piece or 0))
                if least >= 4:
                    act.wait_ge(o_mm, u - 3)
                copy(hid_hi[:, k, cols], hidden[:, k % 2, cols]).then_inc(hi_ready, 1)

            def split_next(n, k, par, uses, first=False):
                if k == 1:
                    act.wait_ge(ew_in[par], uses)
                    if not first:
                        act.wait_ge(h2_mm, UPE * n)
                if k == 3 and not first:
                    act.wait_ge(o_mm, UPE * n)
                part = slice((k - 1) * H, k * H)
                copy(w_hi[par][:, part], w_raw[par][:, part]).then_inc(w_split_hi, 1)

            def stages(n, par, last, uses=None):
                for k in range(UPE):
                    u = UPE * n + k
                    silu(u, k, UPE)
                    if k >= 1 and not last:
                        split_next(n, k, 1 - par, uses)
                    high_half(u - 1, (k - 1) % UPE, UPE + k - 1)

            for k in range(1, UPE):
                split_next(0, k, 1, 48, True)
            silu(0, 0, 0)
            high_half(0, 0, 0)
            silu(1, 1, 1)
            high_half(1, 1, 1)
            silu(2, 2, 2)
            silu(3, 3, 3)
            high_half(2, 2, 2)
            with act.Fori(0, E // 2 - 1) as i:
                stages(2 * i + 1, 1, False, 48 * i + 96)
                stages(2 * i + 2, 0, False, 48 * i + 96)
            stages(E - 1, 1, False, 48 * (E // 2 + 1))
            stages(E, 0, True)

            def evac_moe(b, piece=None):
                cols = piece_of(piece)
                act.wait_ge(o_mm, UNITS + PIECES - 1 if b else UNITS - 2)
                copy(moeT[:, b * SEQ + cols.start:b * SEQ + cols.stop], bank[6 + b][:, cols]).then_inc(moe_evac, 1)

            high_half(UNITS - 1, UPE - 1, UNITS - 1, 0)
            evac_moe(0)
            high_half(UNITS - 1, UPE - 1, UNITS - 1, 1)
            for piece in range(PIECES):
                evac_moe(1, piece)

        @block.vector
        def _(dve):
            steps = [0]

            def step(ins):
                steps[0] += 1
                ins.then_inc(dve_step, 1)

            def settle():
                dve.wait_ge(dve_step, steps[0])

            def moments_of(t0, t1):
                for t in range(t0, t1):
                    step(nc.vector.bn_stats(stats[:, t, :], x_tok[:, t, :]))
                settle()
                for t in range(t0, t1):
                    step(nc.vector.bn_aggr(moments[:, t, :], stats[:, t, :]))
                settle()
                nc.vector.tensor_scalar(var_eps[:, t0:t1], moments[:, t0:t1, 1], EPS, None,
                                        ALU.add).then_inc(var_ready, 1)

            def normalise(n, t0, t1):
                dve.wait_ge(rstd_ready, n + 1)
                for t in range(t0, t1):
                    ins = nc.vector.tensor_scalar(xn[:, t, :], x_tok[:, t, :], moments[:, t, 0:1],
                                                  rstd[:, t:t + 1], ALU.subtract, ALU.mult)
                ins.then_inc(xn_ready, 1)

            def half(b):
                return slice(b * SEQ, (b + 1) * SEQ)

            for b in range(BATCH):
                dve.wait_ge(x_in[b], 16)
                moments_of(b * TPB, (b + 1) * TPB)
            normalise(0, 0, TPB)
            normalise(1, TPB, TILES)
            dve.wait_ge(bias_in, 80)
            for b in range(BATCH):
                dve.wait_ge(z_ready, b + 1)
                step(nc.vector.tensor_scalar(decayT[:, half(b)], zT[:, half(b)], -1.0, 1.0, ALU.mult, ALU.add))
                dve.wait_ge(hh_mm, b + 1)
                step(nc.vector.scalar_tensor_tensor(driveT[:, half(b)], h_bank[b][:], bh[:, 0:1], zT[:, half(b)],
                                                    ALU.add, ALU.mult))
                settle()
                nc.vector.tensor_tensor_scan(hT[:, half(b)], decayT[:, half(b)], driveT[:, half(b)], 0.0,
                                             ALU.mult, ALU.add).then_inc(scan_ready, 1)

            def gated(b):
                dve.wait_ge(gate_ready, b + 1)
                dve.wait_ge(scan_ready, b + 1)
                nc.vector.tensor_tensor(yT[:, half(b)], gateT[:, half(b)], hT[:, half(b)],
                                        ALU.mult).then_inc(y_ready, 1)

            def residual1(b):
                tiles = slice(b * TPB, (b + 1) * TPB)
                dve.wait_ge(ytok_mm, b + 1)
                nc.vector.tensor_tensor(x_tok[:, tiles, :], x_tok[:, tiles, :],
                                        h_bank[b][:].rearrange("p (t d) -> p t d", d=D), ALU.add).then_inc(x1_ready, 1)

            def moments1(b):
                dve.wait_ge(x1_ready, b + 1)
                moments_of(b * TPB, (b + 1) * TPB)

            def low_half_a(r):
                dve.wait_ge(prep_evac, r + 1)
                nc.vector.tensor_tensor(A_lo[:, :, r - 8, :],
                                        prep_bank[r][:, 0:CTX_ROWS].rearrange("p (b l) -> p b l", b=BATCH),
                                        f32(A_hi[:, :, r - 8, :]), ALU.subtract).then_inc(prep_lo, 1)

            def low_half_x(b):
                dve.wait_ge(xt_evac, 2 + b + 1)
                nc.vector.tensor_tensor(x_lo[:, half(b)], xt2_bank[b][:], f32(x_hi[:, half(b)]),
                                        ALU.subtract).then_inc(x_lo_ready, 1)

            gated(0)
            residual1(0)
            moments1(0)
            gated(1)
            low_half_a(8)
            normalise(2, 0, TPB)
            for r in range(9, 12):
                low_half_a(r)
            low_half_x(0)
            low_half_a(12)
            low_half_a(13)

            def row_max(t, hh):
                s = 2 * t + hh
                dve.wait_ge(s_mm, s + 1)
                for j in range(2):
                    ins = nc.vector.tensor_reduce(neg_max[:, s, 2 * j:2 * j + 2],
                                                  bank[2 * hh + j][:, 0:2 * CL].rearrange("p (h l) -> p h l", l=CL),
                                                  AX_X, ALU.max, negate=True)
                ins.then_inc(max_ready, 1)

            def inverse(t, hh):
                s = 2 * t + hh
                dve.wait_ge(exp_done, s + 1)
                nc.vector.reciprocal(inv_sum[:, s, :], row_sum[:, s, :]).then_inc(inv_ready, 1)

            def evac_pt(t, g):
                c0, n = GROUPS[g]
                m = rows_of(c0)
                dve.wait_ge(pt_mm, 3 * t + g + 1)
                if g == 1 and t >= 2:
                    dve.wait_ge(pv_mm, t - 1)
                nc.vector.tensor_copy(probsT[0:m, t % 2, c0:c0 + n, :],
                                      bank[5][0:m, 0:n * P].rearrange("p (c d) -> p c d", d=P)).then_inc(pt_evac, 1)

            def residual2(t):
                dve.wait_ge(pv_mm, t + 1)
                dve.wait_ge(bo_added, t // TPB + 1)
                nc.vector.tensor_tensor(x_tok[:, t, :], x_tok[:, t, :], bank[6 + t % 2][:, 0:D],
                                        ALU.add).then_inc(x2_ready, 1)
                dve.wait_ge(x2_ready, t + 1)
                moments_of(t, t + 1)

            def split_xt3(t):
                cols = slice(t * P, (t + 1) * P)
                dve.wait_ge(xt3_mm, t + 1)
                nc.vector.tensor_copy(x_hi[:, cols], bank[4 + (t == TILES - 1)][:, 0:P]).then_inc(xt3_hi, 1)
                dve.wait_ge(xt3_hi, t + 1)
                nc.vector.tensor_tensor(x_lo[:, cols], bank[4 + (t == TILES - 1)][:, 0:P], f32(x_hi[:, cols]),
                                        ALU.subtract).then_inc(xt3_lo, 1)

            def top2(t):
                dve.wait_ge(logit_mm, t + 1)
                nc.vector.tensor_reduce(logits[:, t, :],
                                        bank[6 + t % 2][:, D:D + 2 * E].rearrange("p (a e) -> p e a", a=2),
                                        AX_X, ALU.add).then_inc(logit_read, 1)
                dve.wait_ge(logit_read, t + 1)
                step(nc.vector.max(top_v[:, t, :], logits[:, t, :]))
                settle()
                step(nc.vector.max_index(top_i[:, t, :], top_v[:, t, :], logits[:, t, :]))

            def gap_of(b):
                tiles = slice(b * TPB, (b + 1) * TPB)
                settle()
                nc.vector.tensor_tensor(gap[:, b, :], top_v[:, tiles, 1], top_v[:, tiles, 0],
                                        ALU.subtract).then_inc(gap_ready, 1)

            def route_shares(b):
                tiles = slice(b * TPB, (b + 1) * TPB)

                def experts(ap):
                    return ap.unsqueeze(1).broadcast_to([P, E, TPB])

                ids = expert_ids[:].unsqueeze(2).broadcast_to([P, E, TPB])
                dve.wait_ge(consts, 6)
                for mask, place in ((mask1, 0), (mask2, 1)):
                    step(nc.vector.tensor_tensor(mask[:, b], ids, experts(top_i[:, tiles, place]), ALU.is_equal))
                dve.wait_ge(second_ready, b + 1)
                step(nc.vector.tensor_scalar(norm1[:, b, :], second[:, b, :], 1.0, None, ALU.add))
                settle()
                step(nc.vector.reciprocal(p1[:, b, :], norm1[:, b, :]))
                settle()
                step(nc.vector.tensor_tensor(p2[:, b, :], second[:, b, :], p1[:, b, :], ALU.mult))
                step(nc.vector.tensor_tensor(mask1[:, b], mask1[:, b], experts(p1[:, b, :]), ALU.mult))
                settle()
                step(nc.vector.tensor_tensor(mask2[:, b], mask2[:, b], experts(p2[:, b, :]), ALU.mult))
                settle()
                nc.vector.tensor_tensor(w_tok[:, b], mask1[:, b], mask2[:, b], ALU.add).then_inc(w_tok_ready, 1)

            def evac_shares(b):
                dve.wait_ge(w_mm, b + 1)
                nc.vector.tensor_copy(w_rows[:, b, :], bank[4][0:E * TPB, 0:P]).then_inc(w_rows_ready, 1)

            def gated_up(u, k, least, piece=None):
                cols = piece_of(piece)
                dve.wait_ge(sil_ready, u + 1)
                dve.wait_ge(h2_mm, u + 1)
                if least >= 2:
                    dve.wait_ge(hid_ready, u - 1)
                nc.vector.tensor_tensor(prod[:, k % 2, cols], sil[:, k % 2, cols], bank[2 + k % 2][:, cols],
                                        ALU.mult).then_inc(prod_ready, 1)

            def low_half(u, k, piece=None):
                cols = piece_of(piece)
                dve.wait_ge(hi_ready, u + 1 + (piece or 0))
                nc.vector.tensor_tensor(hid_lo[:, k, cols], hidden[:, k % 2, cols], f32(hid_hi[:, k, cols]),
                                        ALU.subtract).then_inc(lo_ready, 1)

            def split_next(n, k, par):
                dve.wait_ge(w_split_hi, 3 * n + k)
                part = slice((k - 1) * H, k * H)
                nc.vector.tensor_tensor(w_lo[par][:, part], w_raw[par][:, part], f32(w_hi[par][:, part]),
                                        ALU.subtract).then_inc(w_split_lo, 1)

            low_half_a(14)
            row_max(0, 0)
            low_half_a(15)
            residual1(1)
            row_max(0, 1)
            inverse(0, 0)
            moments1(1)
            inverse(0, 1)
            row_max(1, 0)
            row_max(1, 1)
            inverse(1, 0)
            for t in range(TILES - 1):
                evac_pt(t, 1)
                inverse(t + 1, 1)
                if t + 2 < TILES:
                    row_max(t + 2, 0)
                if t >= 2:
                    normalise(2 * BATCH + t - 2, t - 2, t - 1)
                evac_pt(t, 2)
                if t >= 2:
                    split_xt3(t - 2)
                if t == 0:
                    normalise(3, TPB, TILES)
                if t == 1:
                    low_half_x(1)
                if t + 2 < TILES:
                    row_max(t + 2, 1)
                    inverse(t + 2, 0)
                if t >= 1:
                    residual2(t - 1)
                if t >= 2:
                    top2(t - 2)
                if t == TILES - 3:
                    gap_of(0)
            evac_pt(TILES - 1, 1)
            normalise(2 * BATCH + TILES - 3, TILES - 3, TILES - 2)
            evac_pt(TILES - 1, 2)
            split_xt3(TILES - 3)
            residual2(TILES - 2)
            top2(TILES - 3)
            route_shares(0)
            normalise(2 * BATCH + TILES - 2, TILES - 2, TILES - 1)
            gated_up(0, 0, 0)
            residual2(TILES - 1)
            split_xt3(TILES - 2)
            normalise(2 * BATCH + TILES - 1, TILES - 1, TILES)
            top2(TILES - 2)
            split_xt3(TILES - 1)
            gated_up(1, 1, 1)
            evac_shares(0)
            low_half(0, 0)
            top2(TILES - 1)
            gap_of(1)
            low_half(1, 1)
            gated_up(2, 2, 2)
            route_shares(1)
            gated_up(3, 3, 3)
            evac_shares(1)
            low_half(2, 2)

            def stages(n, par, last):
                for k in range(UPE):
                    u = UPE * n + k
                    if last and k == UPE - 1:
                        for piece in range(PIECES):
                            gated_up(u, k, UPE, piece)
                    else:
                        gated_up(u, k, UPE)
                    low_half(u - 1, (k - 1) % UPE)
                    if k >= 1 and not last:
                        split_next(n, k, 1 - par)

            with dve.Fori(0, E // 2 - 1) as i:
                stages(2 * i + 1, 1, False)
                stages(2 * i + 2, 0, False)
            stages(E - 1, 1, False)
            stages(E, 0, True)

            def residual3(b, piece=None):
                cols = piece_of(piece)
                tiles = slice(b * TPB + cols.start // P, b * TPB + cols.stop // P)
                done = b + 1 + (piece or 0)
                dve.wait_ge(fin_mm, done)
                nc.vector.tensor_tensor(x_tok[:, tiles, :], x_tok[:, tiles, :],
                                        bank[3 + done][:, 0:cols.stop - cols.start].rearrange("p (t d) -> p t d", d=D),
                                        ALU.add).then_inc(out_ready, 1)

            for piece in range(PIECES):
                low_half(UNITS - 1, UPE - 1, piece)
            residual3(0)
            for piece in range(PIECES):
                residual3(1, piece)

        @block.tensor
        def _(pe):
            pe.wait_ge(consts, 6)
            for _ in range(WAKE):
                nc.tensor.matmul(bank[7][:], zeros[:, 0:P], zeros[:], start=True, stop=True)

            def turn(dst, src, n=P):
                return nc.tensor.transpose(dst, src, ident[0:n, 0:n])

            def prep_wait(r):
                if r == 12:
                    pe.wait_ge(gate_ready, 2)
                elif r == 13:
                    pe.wait_ge(x1_ready, 1)
                elif r >= 14:
                    pe.wait_ge(prep_lo, r - 11)
                elif r >= 4:
                    pe.wait_ge(prep_evac, r - 3)

            def turn_weight(r, w, loaded, n):
                pe.wait_ge(loaded, 16)
                for c in range(4):
                    ins = turn(bank[r][:, c * n:(c + 1) * n], w[:, c * P:(c + 1) * P], n)
                ins.then_inc(prep_mm, 1)

            def merge(r, wT, w, evacs):
                pe.wait_ge(prep_evac, evacs)
                prep_wait(r)
                rows = slice((r % 2) * DH, (r % 2 + 1) * DH)
                for i in range(HPU):
                    ins = nc.tensor.matmul(prep_bank[r][0:CTX, i * D:(i + 1) * D], wT[rows, i, :],
                                           w[rows, i, :], start=True, stop=True)
                ins.then_inc(prep_mm, 1)

            def project_a(r):
                prep_wait(r)
                if r == 8:
                    pe.wait_ge(prep_evac, 6)
                nc.tensor.matmul(prep_bank[r][:, 0:CTX_ROWS], M[:, r - 8, :], ctxT[:],
                                 start=True, stop=True).then_inc(prep_mm, 1)

            def project_u(r):
                dst = u_bank[r - 16]
                if r < 18:
                    pe.wait_ge(x_lo_ready, 1)
                    if r == 17:
                        pe.wait_ge(prep_lo, 6)
                elif r < 21:
                    pe.wait_ge(prep_evac, 17 if r == 18 else r)
                else:
                    pe.wait_ge(x_lo_ready, 2)
                if r == 16:
                    pe.wait_ge(prep_evac, 8)
                if r == 18:
                    last = ctxT[:].rearrange("p (b l) -> p b l", b=BATCH)[:, :, P:CL]
                    for h in range(HEADS):
                        n = BATCH * REST
                        ins = nc.tensor.matmul(dst[:, h * n:(h + 1) * n].rearrange("p (b l) -> p b l", b=BATCH),
                                               N[:, h, :], last, start=True, stop=True)
                elif r == 19:
                    m = HPU * REST
                    for q in range(2 * BATCH):
                        b, c = divmod(q, 2)
                        ins = turn(dst[0:m, q * D:(q + 1) * D],
                                   UT_rest[:, b, c * HPU:(c + 1) * HPU, :].rearrange("p h l -> p (h l)"))
                else:
                    b, g = (r - 16) // 4, r % 2
                    ins = nc.tensor.matmul(dst[:], ctxT[:, b * CL:b * CL + P],
                                           N[:, g * HPU:(g + 1) * HPU, :].rearrange("p h d -> p (h d)"),
                                           start=True, stop=True)
                ins.then_inc(prep_mm, 1)

            def turn_tiles(n, b):
                pe.wait_ge(xn_ready, n + 1)
                if n == 2:
                    pe.wait_ge(gate_ready, 1)
                if n == 3:
                    pe.wait_ge(prep_evac, 18)
                dst = bank[4 + b] if n < 2 else xt2_bank[b]
                for t in range(TPB):
                    ins = turn(dst[:, t * P:(t + 1) * P], xn[:, b * TPB + t, :])
                ins.then_inc(xt_mm, 1)

            def gate_inputs(b):
                cols = slice(b * SEQ, (b + 1) * SEQ)
                pe.wait_ge(wzh_in, 64)
                pe.wait_ge(xt_evac, b + 1)
                nc.tensor.matmul(z_bank[b][:], wz[:], xnT[:, cols], start=True, stop=True).then_inc(z_mm, 1)
                nc.tensor.matmul(h_bank[b][:], wh[:], xnT[:, cols], start=True, stop=True).then_inc(hh_mm, 1)

            def out_gate(b):
                if b == 0:
                    pe.wait_ge(wg_in, 16)
                pe.wait_ge(z_ready, b + 1)
                pe.wait_ge(scan_ready, b + 1)
                nc.tensor.matmul(z_bank[b][:], wg[:], hT[:, b * SEQ:(b + 1) * SEQ],
                                 start=True, stop=True).then_inc(gate_mm, 1)

            def turn_y(b):
                pe.wait_ge(y_ready, b + 1)
                pe.wait_ge(scan_ready, b + 1)
                for t in range(TPB):
                    ins = turn(h_bank[b][:, t * P:(t + 1) * P], yT[:, b * SEQ + t * P:b * SEQ + (t + 1) * P])
                ins.then_inc(ytok_mm, 1)

            pe.wait_ge(ctx_in_s, 16)
            for c in range(CTX_CUT):
                ins = turn(bank[0][0:CTX, c * CTX_TILE:(c + 1) * CTX_TILE], ctx_rows[:, c, :], CTX_TILE)
            ins.then_inc(prep_mm, 1)
            turn_weight(1, wk, wk_in, CTX)
            turn_weight(2, wq, wq_in, P)
            turn_tiles(0, 0)
            turn_weight(3, wv, wv_in, CTX)
            gate_inputs(0)
            turn_tiles(1, 1)
            merge(4, wkT, wqT, 3)
            gate_inputs(1)
            out_gate(0)
            merge(5, wkT, wqT, 3)
            pe.wait_ge(wo_in, 16)
            merge(6, wvT, wo, 4)
            turn_y(0)
            out_gate(1)
            merge(7, wvT, wo, 4)
            project_a(8)
            project_a(9)
            project_a(10)
            turn_y(1)
            project_a(11)
            project_a(12)
            turn_tiles(2, 0)
            for r in range(13, 16):
                project_a(r)

            def scores(t, hh):
                s = 2 * t + hh
                if t >= 1:
                    pe.wait_ge(exp_done, s - 1)
                else:
                    pe.wait_ge(prep_lo, 4 + 4 * hh)
                if t % TPB == 0 and hh == 0:
                    pe.wait_ge(x_lo_ready, 1 + t // TPB)
                cols = slice(t * P, (t + 1) * P)
                for j in range(2):
                    h0 = hh * HPU + 2 * j
                    rhs = [a[:, t // TPB, h0:h0 + 2, :].rearrange("p h l -> p (h l)") for a in (A_hi, A_lo)]
                    ins = split_product(nc, bank[2 * hh + j][:, 0:2 * CL], (x_hi[:, cols], x_lo[:, cols]), rhs)
                ins.then_inc(s_mm, 1)

            def turn_probs(t, g):
                if g < 2:
                    pe.wait_ge(pn_ready, 2 * t + g + 1)
                if g == 0:
                    if t == 0:
                        pe.wait_ge(gate_ready, 2)
                    if t >= 1:
                        pe.wait_ge(pt0_evac, t)
                    if t >= 3:
                        pe.wait_ge(xt3_lo, t - 2)
                if g == 1:
                    if t == 0:
                        pe.wait_ge(x1_ready, 2)
                    else:
                        pe.wait_ge(pt_evac, 2 * t)
                if g == 2:
                    pe.wait_ge(pt_evac, 2 * t + 1)
                c0, n = GROUPS[g]
                for c in range(c0, c0 + n):
                    m = rows_of(c)
                    ins = turn(bank[4 if g == 0 else 5][0:m, (c - c0) * P:(c - c0) * P + P],
                               probs_n[:, t % 2, pairs_of(c)])
                ins.then_inc(pt_mm, 1)

            def turn_tile3(t):
                pe.wait_ge(xn_ready, 4 + t + 1)
                if t < TILES - 1:
                    pe.wait_ge(pt0_evac, min(t + 3, TILES))
                    turn(bank[4][:, 0:P], xn[:, t, :]).then_inc(xt3_mm, 1)
                else:
                    pe.wait_ge(pt_evac, 2 * TILES)
                    turn(bank[5][:, 0:P], xn[:, t, :]).then_inc(xt3_mm, 1)

            def attend(t, chunks):
                for c in chunks:
                    if c == 0:
                        if t < 2:
                            pe.wait_ge(prep_evac, PREP - 1 + t)
                        if t >= 2:
                            pe.wait_ge(x2_ready, t - 1)
                            pe.wait_ge(logit_read, t - 1)
                        pe.wait_ge(pt0_evac, t + 1)
                    if c in (4, 8):
                        pe.wait_ge(pt_evac, 2 * t + c // 4)
                    m = rows_of(c)
                    ins = nc.tensor.matmul(bank[6 + t % 2][:, 0:D], probsT[0:m, t % 2, c, :],
                                           U[0:m, t // TPB, c, :], start=(c == 0), stop=(c == NCH - 1))
                if chunks[-1] == NCH - 1:
                    ins.then_inc(pv_mm, 1)

            def route(t):
                if t == 0:
                    pe.wait_ge(gw_split, 2)
                pe.wait_ge(xt3_lo, t + 1)
                pe.wait_ge(x2_ready, t + 1)
                cols = slice(t * P, (t + 1) * P)
                nc.tensor.matmul(bank[6 + t % 2][:, D:D + 2 * E], x_hi[:, cols], gw[:], start=True, stop=False,
                                 skip_group_check=True)
                nc.tensor.matmul(bank[6 + t % 2][:, D:D + E], x_lo[:, cols], gw[:, 0:E], start=False, stop=True,
                                 skip_group_check=True).then_inc(logit_mm, 1)

            def up(u, k, par, least):
                n, c = k // HC, k % HC
                cols = slice(n * SEQ, (n + 1) * SEQ)
                if least >= 2:
                    pe.wait_ge(sil_ready, u - 1)
                    pe.wait_ge(prod_ready, u - 1)
                for w0, dst, done in ((0, bank[k % 2], h1_mm), (H, bank[2 + k % 2], h2_mm)):
                    part = slice(w0 + c * P, w0 + (c + 1) * P)
                    split_product(nc, dst[:], (w_hi[par][:, part], w_lo[par][:, part]),
                                  (x_hi[:, cols], x_lo[:, cols])).then_inc(done, 1)

            def turn_shares(b):
                pe.wait_ge(w_tok_ready, b + 1)
                if b == 0:
                    pe.wait_ge(xt3_lo, TILES - 1)
                else:
                    pe.wait_ge(w_rows_ready, 1)
                turn(bank[4][0:E * TPB, 0:P], w_tok[:, b].rearrange("p e t -> p (e t)")).then_inc(w_mm, 1)

            def open_sum(n):
                nc.tensor.matmul(bank[6 + n][:], zeros[:, 0:P], zeros[:], start=True, stop=False,
                                 skip_group_check=True)

            def down(u, k, par, piece=None):
                n, c = k // HC, k % HC
                part = slice(2 * H + c * P, 2 * H + (c + 1) * P)
                cols = piece_of(piece)
                pe.wait_ge(lo_ready, u + 1 + (piece or 0))
                split_product(nc, bank[6 + n][:, cols], (w_hi[par][:, part], w_lo[par][:, part]),
                              (hid_hi[:, k, cols], hid_lo[:, k, cols]), start=False, stop=False,
                              skip_group_check=True).then_inc(o_mm, 1)

            scores(0, 0)
            project_u(16)
            project_u(17)
            scores(0, 1)
            scores(1, 0)
            project_u(18)
            scores(1, 1)
            for t in range(TILES - 1):
                turn_probs(t, 0)
                turn_probs(t, 1)
                if t == 1:
                    turn_tiles(3, 1)
                if t == 0:
                    project_u(19)
                if t + 2 < TILES:
                    scores(t + 2, 0)
                if t >= 1:
                    attend(t - 1, range(0, 5))
                turn_probs(t, 2)
                if t + 2 < TILES:
                    scores(t + 2, 1)
                if t >= 2:
                    turn_tile3(t - 2)
                if t == 0:
                    project_u(20)
                if t >= 1:
                    attend(t - 1, range(5, NCH))
                if t == 1:
                    project_u(21)
                if t >= 2:
                    route(t - 2)
            turn_probs(TILES - 1, 0)
            turn_probs(TILES - 1, 1)
            attend(TILES - 2, range(0, 5))
            turn_probs(TILES - 1, 2)
            turn_tile3(TILES - 3)
            attend(TILES - 2, range(5, NCH))
            route(TILES - 3)
            pe.wait_ge(first_lo, 1)
            pe.wait_ge(exp_done, 2 * TILES)
            up(0, 0, 0, 0)
            attend(TILES - 1, range(NCH))
            turn_tile3(TILES - 2)
            up(1, 1, 0, 1)
            route(TILES - 2)
            turn_tile3(TILES - 1)
            turn_shares(0)
            pe.wait_ge(logit_read, TILES - 1)
            open_sum(0)
            route(TILES - 1)
            up(2, 2, 0, 2)
            pe.wait_ge(logit_read, TILES)
            open_sum(1)
            down(0, 0, 0)
            up(3, 3, 0, 3)

            def stages(n, par, thirds, shares_after=None):
                for k in range(UPE):
                    u = UPE * n + k
                    if k == 0:
                        pe.wait_ge(w_split_lo, thirds + 2)
                    up(u, k, par, UPE)
                    if shares_after == k:
                        turn_shares(1)
                    if k == 3:
                        pe.wait_ge(w_split_lo, thirds + 3)
                    down(u - 3, (k - 3) % UPE, par if k == 3 else 1 - par)

            stages(1, 1, 0, shares_after=0)
            with pe.Fori(0, E // 2 - 1) as i:
                stages(2 * i + 2, 0, 6 * i + 3)
                stages(2 * i + 3, 1, 6 * i + 6)
            stages(E, 0, 3 * (E - 1))

            def turn_moe(b, piece=None):
                cols = piece_of(piece)
                done = b + 1 + (piece or 0)
                pe.wait_ge(moe_evac, done)
                for t in range(cols.start // P, cols.stop // P):
                    col = t * P - cols.start
                    ins = turn(bank[3 + done][:, col:col + P], moeT[:, b * SEQ + t * P:b * SEQ + (t + 1) * P])
                ins.then_inc(fin_mm, 1)

            down(UNITS - 3, 1, 0)
            down(UNITS - 2, 2, 0)
            pe.wait_ge(w_rows_ready, BATCH)
            turn_moe(0)
            for piece in range(PIECES):
                down(UNITS - 1, 3, 0, piece)
            for piece in range(PIECES):
                turn_moe(1, piece)


_INS = ["x", "ctx_768", "L0_attn_W_zf", "L0_attn_b_zf", "L0_attn_W_hf", "L0_attn_b_hf", "L0_attn_W_zs",
        "L0_attn_b_zs", "L0_attn_W_hs", "L0_attn_b_hs", "L0_attn_W_g", "L0_attn_b_g", "L0_xattn_Wq",
        "L0_xattn_Wk", "L0_xattn_Wv", "L0_xattn_Wo", "L0_xattn_bo", "L0_ffn_gate_w", "L0_ffn_ew1",
        "L0_ffn_ew2", "L0_ffn_ew3", "L0_ffn_sw1", "L0_ffn_sw2", "L0_ffn_sw3"]


def kernel(**inputs):
    import numpy as _np
    import concourse.bacc as _bacc
    from concourse import mybir as _mybir
    from concourse.bass_utils import run_bass_kernel_spmd as _run

    nc = _bacc.Bacc("TRN2", target_bir_lowering=False, num_devices=1)
    arrays, args = {}, []
    for name in _INS:
        a = _np.ascontiguousarray(inputs[name])
        arrays[f"in_{name}"] = a
        args.append(nc.dram_tensor(f"in_{name}", a.shape, _mybir.dt.from_np(a.dtype), kind="ExternalInput").ap())
    args.append(nc.dram_tensor("router_scratch", (2, 8, 512), _mybir.dt.float32).ap())
    args.append(nc.dram_tensor("out_0", (2, 512, 128), _mybir.dt.float32, kind="ExternalOutput").ap())
    decoder_block(nc, *args)
    return _run(nc, [arrays], core_ids=[0]).results[0]["out_0"]
```
